# Optimizing a Trainium2 kernel written in Bass

```python
import numpy as np
import jax
import jax.numpy as jnp

def _softmax(x, axis=-1):
    return jax.nn.softmax(x, axis=axis)

def _gelu(x):
    return jax.nn.gelu(x, approximate=True)

def _silu(x):
    return jax.nn.silu(x)

def _sigmoid(x):
    return jax.nn.sigmoid(x)

def _layernorm(x, axis=-1, eps=1e-05):
    m = jnp.mean(x, axis=axis, keepdims=True)
    v = jnp.var(x, axis=axis, keepdims=True)
    return (x - m) / jnp.sqrt(v + eps)

def _scatter_add(tgt, idx, src, axis=0):
    return tgt.at[idx].add(src)

def _segment_sum(src, seg, n):
    return jax.ops.segment_sum(src, seg, n)
kernel_name = 'mk_xattn_ffn_d1_seqx_r4_e00080'

def setup_inputs(seed: int=0):
    np.random.seed(seed)
    _w = jnp.asarray

    def _rec_inputs():
        import jax
        import jax.numpy as jnp
        _rk = jax.random.key(seed)
        x = 0.0003765 + 1 * jax.random.normal(jax.random.fold_in(_rk, 1), (16, 256, 512), jnp.float32)
        _lenS = 256 - jax.random.randint(jax.random.fold_in(_rk, 7), (16,), 0, max(1, 256 // 4) + 1, jnp.int32)
        _lenS2 = 256 - jax.random.randint(jax.random.fold_in(_rk, 8), (16,), 0, max(1, 256 // 4) + 1, jnp.int32)
        _ctx_2048P = jax.random.normal(jax.random.fold_in(_rk, 11), (16, 16, 512), jnp.float32)
        _ctx_2048c = jax.random.dirichlet(jax.random.fold_in(_rk, 511), 0.3 * jnp.ones((16,), jnp.float32), (16, 256))
        _ctx_2048t = jnp.einsum('bsk,bkd->bsd', _ctx_2048c, _ctx_2048P)
        _ctx_2048t = _ctx_2048t * jax.lax.rsqrt(jnp.mean(jnp.square(_ctx_2048t)) + 1e-12) * 0.953939
        ctx_2048 = -0.000292821 + 1.00034 * (_ctx_2048t + 0.3 * jax.random.normal(jax.random.fold_in(_rk, 611), (16, 256, 512), jnp.float32))
        return (x, ctx_2048)
    x, ctx_2048 = _rec_inputs()

    def _L0_xattn_setup():
        import jax, jax.numpy as jnp
        import numpy as np
        key = jax.random.key(seed)
        k1, k2, k3, k4, k5 = jax.random.split(key, 5)
        B, D_MODEL, L = (2, 256, 512)
        HEAD_DIM = 8
        H = D_MODEL // HEAD_DIM
        return {'k': jax.random.normal(k1, (B, D_MODEL, L), dtype=jnp.float32), 'v': jax.random.normal(k2, (B, D_MODEL, L), dtype=jnp.float32), 'q': jax.random.normal(k3, (B, D_MODEL, L), dtype=jnp.float32), 'ssm_kernel': jax.random.normal(k4, (H, L), dtype=jnp.float32), 'D': jax.random.normal(k5, (H,), dtype=jnp.float32), 'head_dim': HEAD_DIM}
    _L0_xattn_all = _L0_xattn_setup()
    _L0_xattn_in = {k: v for k, v in _L0_xattn_all.items() if k in ('ssm_kernel', 'D')}
    del _L0_xattn_all

    def _L0_ffn_setup():
        import jax, jax.numpy as jnp
        import numpy as np
        B, S, D = (4, 128, 512)
        E, K, H = (8, 2, 352)
        HS = 2 * 352
        ALPHA = 0.001
        W_SCALE = 0.02

        def _moe_forward(hidden_states, gate_w, w_gate, w_up, w_down, sw_gate, sw_up, sw_down):
            b, s, d = hidden_states.shape
            x = hidden_states.reshape(-1, d)
            T = x.shape[0]
            logits = x @ gate_w
            scores = jax.nn.softmax(logits, axis=-1)
            topk_w, topk_idx = jax.lax.top_k(scores, K)
            mask = jax.nn.one_hot(topk_idx, E, dtype=scores.dtype).sum(axis=1)
            ce = mask.mean(axis=0)
            Pi = scores.mean(axis=0)
            aux_loss = (Pi * ce * E).sum() * ALPHA
            comb = jnp.zeros((T, E), dtype=x.dtype)
            comb = comb.at[jnp.arange(T)[:, None], topk_idx].add(topk_w)
            g = jax.nn.silu(jnp.einsum('td,edh->teh', x, w_gate)) * jnp.einsum('td,edh->teh', x, w_up)
            routed = jnp.einsum('teh,ehd,te->td', g, w_down, comb)
            shared = jax.nn.silu(x @ sw_gate) * (x @ sw_up) @ sw_down
            out = (routed + shared).reshape(b, s, d)
            return (out, aux_loss)
        key = jax.random.key(seed)
        ks = jax.random.split(key, 8)
        rn = lambda k, sh: jax.random.normal(k, sh, dtype=jnp.float32)
        return {'hidden_states': rn(ks[0], (B, S, D)), 'gate_w': rn(ks[1], (D, E)) * W_SCALE, 'w_gate': rn(ks[2], (E, D, H)) * W_SCALE, 'w_up': rn(ks[3], (E, D, H)) * W_SCALE, 'w_down': rn(ks[4], (E, H, D)) * W_SCALE, 'sw_gate': rn(ks[5], (D, HS)) * W_SCALE, 'sw_up': rn(ks[6], (D, HS)) * W_SCALE, 'sw_down': rn(ks[7], (HS, D)) * W_SCALE}
    _L0_ffn_all = _L0_ffn_setup()
    _L0_ffn_in = {k: v for k, v in _L0_ffn_all.items() if k in ('gate_w', 'w_gate', 'w_up', 'w_down', 'sw_gate', 'sw_up', 'sw_down')}
    del _L0_ffn_all
    return {'x': x, 'ctx_2048': ctx_2048, 'L0_xattn_ssm_kernel': _L0_xattn_in['ssm_kernel'], 'L0_xattn_D': _L0_xattn_in['D'], 'L0_ffn_gate_w': _L0_ffn_in['gate_w'], 'L0_ffn_w_gate': _L0_ffn_in['w_gate'], 'L0_ffn_w_up': _L0_ffn_in['w_up'], 'L0_ffn_w_down': _L0_ffn_in['w_down'], 'L0_ffn_sw_gate': _L0_ffn_in['sw_gate'], 'L0_ffn_sw_up': _L0_ffn_in['sw_up'], 'L0_ffn_sw_down': _L0_ffn_in['sw_down']}

def reference(x, ctx_2048, L0_xattn_ssm_kernel, L0_xattn_D, L0_ffn_gate_w, L0_ffn_w_gate, L0_ffn_w_up, L0_ffn_w_down, L0_ffn_sw_gate, L0_ffn_sw_up, L0_ffn_sw_down):
    import jax
    import jax.numpy as jnp

    def _L0_xattn_ref(k, v, q, ssm_kernel, D, head_dim):
        import jax, jax.numpy as jnp
        import numpy as np
        B, HD, L = k.shape
        H = HD // head_dim
        fft_size = 2 * L
        k_ = k.reshape(B, H, head_dim, L)
        v_ = v.reshape(B, H, head_dim, L)
        q_ = q.reshape(B, H, head_dim, L)
        kv = jnp.einsum('bhil,bhjl->bijhl', k_, v_)
        kv_f = jnp.fft.rfft(kv, n=fft_size)
        kernel_f = jnp.fft.rfft(ssm_kernel, n=fft_size)
        y = jnp.fft.irfft(kv_f * kernel_f, n=fft_size)[..., :L]
        out = y + kv * D[None, None, None, :, None]
        out = jnp.einsum('bijhl,bhil->bjhl', out, q_)
        out = jnp.transpose(out, (0, 2, 1, 3)).reshape(B, H * head_dim, L)
        return out.astype(k.dtype)

    def _L0_ffn_ref(hidden_states, gate_w, w_gate, w_up, w_down, sw_gate, sw_up, sw_down):
        import jax, jax.numpy as jnp
        import numpy as np
        B, S, D = (4, 128, 512)
        E, K, H = (8, 2, 352)
        HS = 2 * 352
        ALPHA = 0.001
        W_SCALE = 0.02

        def _moe_forward(hidden_states, gate_w, w_gate, w_up, w_down, sw_gate, sw_up, sw_down):
            b, s, d = hidden_states.shape
            x = hidden_states.reshape(-1, d)
            T = x.shape[0]
            logits = x @ gate_w
            scores = jax.nn.softmax(logits, axis=-1)
            topk_w, topk_idx = jax.lax.top_k(scores, K)
            mask = jax.nn.one_hot(topk_idx, E, dtype=scores.dtype).sum(axis=1)
            ce = mask.mean(axis=0)
            Pi = scores.mean(axis=0)
            aux_loss = (Pi * ce * E).sum() * ALPHA
            comb = jnp.zeros((T, E), dtype=x.dtype)
            comb = comb.at[jnp.arange(T)[:, None], topk_idx].add(topk_w)
            g = jax.nn.silu(jnp.einsum('td,edh->teh', x, w_gate)) * jnp.einsum('td,edh->teh', x, w_up)
            routed = jnp.einsum('teh,ehd,te->td', g, w_down, comb)
            shared = jax.nn.silu(x @ sw_gate) * (x @ sw_up) @ sw_down
            out = (routed + shared).reshape(b, s, d)
            return (out, aux_loss)
        out, _aux = _moe_forward(hidden_states, gate_w, w_gate, w_up, w_down, sw_gate, sw_up, sw_down)
        return out
    x = x + _L0_xattn_ref(ctx_2048, ctx_2048, _layernorm(x, axis=-1), L0_xattn_ssm_kernel, L0_xattn_D, 8)
    x = x + _L0_ffn_ref(_layernorm(x, axis=-1), L0_ffn_gate_w, L0_ffn_w_gate, L0_ffn_w_up, L0_ffn_w_down, L0_ffn_sw_gate, L0_ffn_sw_up, L0_ffn_sw_down)
    return x

_drawn_inputs = setup_inputs


def setup_inputs(seed=0):
    import zlib

    import numpy as np

    out = dict(_drawn_inputs(seed))
    spreads = {}
    factors = {'L0_ffn_gate_w': 8.0,
     'L0_ffn_w_gate': 8.0,
     'L0_ffn_w_up': 8.0,
     'L0_ffn_w_down': 8.0,
     'L0_ffn_sw_gate': 8.0,
     'L0_ffn_sw_up': 8.0,
     'L0_ffn_sw_down': 8.0}
    for name, (base, spread) in spreads.items():
        noise = np.random.default_rng([zlib.crc32(name.encode()), seed]).standard_normal(out[name].shape)
        drawn = base * np.exp(spread * noise) if base else spread * noise
        out[name] = jnp.asarray(drawn.astype(out[name].dtype))
    for name, factor in factors.items():
        out[name] = (out[name] * factor).astype(out[name].dtype)
    return out
```

```python
from contextlib import ExitStack

import concourse.bass as bass
from concourse import mybir

F32 = mybir.dt.float32
F32R = mybir.dt.float32r
F16 = mybir.dt.float16
I32 = mybir.dt.int32
U32 = mybir.dt.uint32
ALU = mybir.AluOpType
ACT = mybir.ActivationFunctionType
AX = mybir.AxisListType

P = 128
EPS = 1e-5


def shapes_of(x, ssm_kernel, gate_w, w_gate):
    s = {}
    s["B"], s["CH"], s["L"] = x.shape
    s["H"] = ssm_kernel.shape[0]
    s["HD"] = s["CH"] // s["H"]
    s["E"], _, s["F"] = w_gate.shape
    s["LB"] = s["L"] // P
    s["HALVES"] = s["CH"] // P
    s["HEADS_PER_TILE"] = P // s["HD"]
    s["TOKENS"] = s["B"] * s["CH"]
    s["TILES"] = s["TOKENS"] // P
    return s


def identities(nc, s, ctx):
    ident = ctx.enter_context(nc.sbuf_tensor("ident", [P, P], F32))
    ident16 = ctx.enter_context(nc.sbuf_tensor("ident16", [P, P], F16))
    zeroed = ctx.enter_context(nc.semaphore("ident_zeroed"))
    drawn = ctx.enter_context(nc.semaphore("ident_drawn"))
    with nc.Block() as block:

        @block.gpsimd
        def _(pool):
            pool.memset(ident[:, :], 0.0).then_inc(zeroed, 1)
            pool.wait_ge(zeroed, 1)
            pool.affine_select(out=ident[:, :], in_=ident[:, :], compare_op=ALU.not_equal, fill=1.0,
                               base=0, pattern=[[-1, P]], channel_multiplier=1).then_inc(drawn, 1)

        @block.vector
        def _(dve):
            dve.wait_ge(drawn, 1)
            dve.tensor_copy(ident16[:, :], ident[:, :]).then_inc(zeroed, 1)
    s["passed"] = ctx.enter_context(nc.semaphore("waits_passed"))
    return ident, ident16


def pass_waits(eng, s):
    eng.sem_inc(s["passed"], 1)


def prologue(nc, s, x, ctx_in, ssm_kernel, dvec, kpad, ctxT, qT, ident):
    B, L, LB, H, HD = s["B"], s["L"], s["LB"], s["H"], s["HD"]
    HT = s["HEADS_PER_TILE"]
    with ExitStack() as c:
        sb = lambda n, sh, dt=F32: c.enter_context(nc.sbuf_tensor(n, sh, dt))
        sem = lambda n: c.enter_context(nc.semaphore(n))
        x_in = sb("p_x_in", [P, 2, L])
        c_in = sb("p_c_in", [P, 2, L])
        c_rev = sb("p_c_rev", [P, 2, L])
        qn = sb("p_qn", [P, 2, L])
        stats = sb("p_stats", [P, 2, 6])
        moments = sb("p_moments", [P, 2, 2])
        rstd = sb("p_rstd", [P, 2, 1])
        var_eps = sb("p_var_eps", [P, 2, 1])
        power = sb("p_power", [P, 1])
        kp = sb("p_kpad", [H, P + L])
        dcol = sb("p_dcol", [H, 1])
        ps_q = c.enter_context(nc.psum_tensor("p_ps_q", [P, 2, LB * P], F32))
        ps_c = c.enter_context(nc.psum_tensor("p_ps_c", [P, 2, LB * P], F32))
        x_loaded = [sem(f"p_x_loaded{u}") for u in range(2)]
        c_loaded = [sem(f"p_c_loaded{u}") for u in range(2)]
        kp_loaded, kp_zeroed, kp_done, kp_stored = sem("kp_loaded"), sem("kp_zeroed"), sem("kp_done"), sem("kp_stored")
        stats_done, moments_done, rstd_done, qn_done = sem("p_stats"), sem("p_moments"), sem("p_rstd"), sem("p_qn")
        c_rev_done, var_eps_done = sem("c_rev_done"), sem("var_eps_done")
        q_turned, c_turned, q_kept, c_kept = sem("q_turned"), sem("c_turned"), sem("q_kept"), sem("c_kept")
        block = c.enter_context(nc.Block())

        @block.sync
        def _(sp):
            sp.dma_start(kp[:, P:P + L], ssm_kernel).then_inc(kp_loaded, 16)
            sp.dma_start(dcol[:, :], dvec.rearrange("(h a) -> h a", a=1)).then_inc(kp_loaded, 16)
            for b0 in range(1):
                for u in range(2):
                    sp.dma_start(x_in[:, u, :], x[b0, u * P:(u + 1) * P, :]).then_inc(x_loaded[u], 16)
                    sp.dma_start(c_in[:, u, :], ctx_in[b0, u * P:(u + 1) * P, :]).then_inc(c_loaded[u], 16)
            with sp.Fori(1, B) as b:
                for u in range(2):
                    sp.wait_ge(qn_done, 2 * b - 1 + u)
                    sp.dma_start(x_in[:, u, :], x[bass.ds(b, 1), u * P:(u + 1) * P, :]
                                 .rearrange("a p l -> (a p) l")).then_inc(x_loaded[u], 16)
                    sp.wait_ge(c_rev_done, 2 * b - 1 + u)
                    sp.dma_start(c_in[:, u, :], ctx_in[bass.ds(b, 1), u * P:(u + 1) * P, :]
                                 .rearrange("a p l -> (a p) l")).then_inc(c_loaded[u], 16)
            sp.wait_ge(kp_done, 1)
            sp.dma_start(kpad[:, :], kp[:, :]).then_inc(kp_stored, 16)
            sp.wait_ge(kp_stored, 16)

        @block.vector
        def _(dve):
            dve.memset(kp[:, 0:P], 0.0).then_inc(kp_zeroed, 1)
            dve.wait_ge(kp_zeroed, 1)
            dve.wait_ge(kp_loaded, 32)
            dve.tensor_tensor(kp[:, P:P + 1], kp[:, P:P + 1], dcol[:, :], ALU.add).then_inc(kp_done, 1)
            with dve.Fori(0, B) as b:
                for u in range(2):
                    n = 2 * b + u + 1
                    dve.wait_ge(x_loaded[u], 16 * b + 16)
                    dve.bn_stats(stats[:, u, :], x_in[:, u, :]).then_inc(stats_done, 1)
                    dve.wait_ge(stats_done, n)
                    pass_waits(dve, s)
                    dve.bn_aggr(moments[:, u, :], stats[:, u, :]).then_inc(moments_done, 1)
                    dve.wait_ge(rstd_done, n)
                    dve.wait_ge(q_turned, n)
                    dve.tensor_scalar(qn[:, u, :], x_in[:, u, :], moments[:, u, 0:1], rstd[:, u, :],
                                      ALU.subtract, ALU.mult).then_inc(qn_done, 1)

        @block.gpsimd
        def _(pool):
            pool.memset(power[:, :], -0.5).then_inc(var_eps_done, 1)
            with pool.Fori(0, B) as b:
                for u in range(2):
                    n = 2 * b + u + 1
                    pool.wait_ge(c_loaded[u], 16 * b + 16)
                    pool.wait_ge(c_turned, n)
                    pass_waits(pool, s)
                    whole = c_in[:, u, L - 1:L]
                    backwards = bass.AP(whole.tensor, whole.offset, [whole.ap[0], [-1, L]])
                    pool.tensor_copy(c_rev[:, u, :], backwards).then_inc(c_rev_done, 1)
                    pool.wait_ge(moments_done, n)
                    pass_waits(pool, s)
                    pool.tensor_scalar(var_eps[:, u, :], moments[:, u, 1:2], EPS, None, ALU.add)\
                        .then_inc(var_eps_done, 1)
                    pool.wait_ge(var_eps_done, n + 1)
                    pool.tensor_tensor(rstd[:, u, :], var_eps[:, u, :], power[:, :], ALU.pow)\
                        .then_inc(rstd_done, 1)

        @block.tensor
        def _(pe):
            pe.sem_inc(c_turned, 2)
            pe.sem_inc(q_turned, 2)
            with pe.Fori(0, B) as b:
                for u in range(2):
                    n = 2 * b + u + 1
                    pe.wait_ge(c_rev_done, n)
                    pe.wait_ge(c_kept, n)
                    for lb in range(LB):
                        src = slice((LB - 1 - lb) * P, (LB - lb) * P)
                        mm = pe.transpose(ps_c[:, u, lb * P:(lb + 1) * P], c_rev[:, u, src], ident[:, :])
                    mm.then_inc(c_turned, 1)
                    pe.wait_ge(qn_done, n)
                    pe.wait_ge(q_kept, n)
                    for lb in range(LB):
                        mm = pe.transpose(ps_q[:, u, lb * P:(lb + 1) * P], qn[:, u, lb * P:(lb + 1) * P], ident[:, :])
                    mm.then_inc(q_turned, 1)

        @block.scalar
        def _(act):
            act.sem_inc(c_kept, 2)
            act.sem_inc(q_kept, 2)
            with act.Fori(0, B) as b:
                for u in range(2):
                    n = 2 * b + u + 1
                    for ps, kept, turned, dst in ((ps_c, c_kept, c_turned, ctxT), (ps_q, q_kept, q_turned, qT)):
                        act.wait_ge(turned, n + 2)
                        act.activation(
                            dst[:, :, bass.ds(b, 1), u * HT:(u + 1) * HT, :].rearrange("p a b h j -> p a (b h j)"),
                            ps[:, u, :].rearrange("p (a t) -> p a t", a=LB), ACT.Copy).then_inc(kept, 1)


def convolve(nc, s, kpad, ctxT, qT):
    B, L, LB, H, HD = s["B"], s["L"], s["LB"], s["H"], s["HD"]
    NP = HD * (HD + 1) // 2
    FULL = HD // 2
    EXT = HD + FULL
    HB = B // 2
    ROWS = LB * B
    with ExitStack() as c:
        sb = lambda n, sh, dt=F32: c.enter_context(nc.sbuf_tensor(n, sh, dt))
        sem = lambda n: c.enter_context(nc.semaphore(n))
        toep = sb("toep", [P, 2, L])
        toep_hi = sb("toep_hi", [P, 2, L], F32R)
        toep_lo = sb("toep_lo", [P, 2, L], F32R)
        kext = sb("kext", [P, 2, ROWS, EXT])
        qext = sb("qext", [P, 2, ROWS, EXT])
        kv = sb("kv", [P, ROWS, NP])
        kv_hi = sb("kv_hi", [P, 2, ROWS, NP], F32R)
        kv_lo = sb("kv_lo", [P, 2, ROWS, NP], F32R)
        prods = sb("prods", [P, 2, B, HD, HD])
        ps = [c.enter_context(nc.psum_tensor(f"ps_y{n}", [P, 2, 512], F32)) for n in range(4)]
        toep_loaded = [sem(f"toep_loaded{u}") for u in range(2)]
        toep_free, toep_hi_done, toep_lo_done = sem("toep_free"), sem("toep_hi_done"), sem("toep_lo_done")
        kext_done, qext_done = sem("kext_done"), sem("qext_done")
        kv_done, kv_hi_done, kv_lo_done = sem("kv_done"), sem("kv_hi_done"), sem("kv_lo_done")
        y_done, prods_done = sem("y_done"), sem("prods_done")
        KV_AHEAD, LO_AHEAD, Y_AHEAD, PRODS_AHEAD, TOEP_AHEAD = 2, 1, 2 * LB, LB + 1, 2
        block = c.enter_context(nc.Block())

        @block.sync
        def _(sp):
            with sp.Fori(0, H // 2) as pair:
                for u in range(2):
                    h = 2 * pair + u
                    sp.wait_ge(toep_free, h + 1)
                    src = bass.AP(kpad, h * (P + L) + 1, [[1, P], [1, L]])
                    sp.dma_start(toep[:, u, :], src).then_inc(toep_loaded[u], 16)

        @block.scalar
        def _(act):
            with act.Fori(0, H // 2) as pair:
                for u in range(2):
                    h = 2 * pair + u
                    n = h + 1
                    k_h, q_h = (a[:, :, :, bass.ds(h, 1), :].rearrange("p a b h j -> p (a b) (h j)") for a in (ctxT, qT))
                    ke, qe = kext[:, u, :, :], qext[:, u, :, :]
                    act.wait_ge(kv_done, n)
                    act.activation(ke[:, :, 0:HD], k_h, ACT.Copy)
                    act.activation(ke[:, :, HD:EXT], k_h[:, :, 0:FULL], ACT.Copy).then_inc(kext_done, 1)
                    act.wait_ge(toep_loaded[u], 16 * pair + 16)
                    act.wait_ge(y_done, LB * n)
                    act.activation(toep_hi[:, u, :], toep[:, u, :], ACT.Copy).then_inc(toep_hi_done, 1)
                    act.wait_ge(prods_done, LB * h + 1)
                    act.activation(qe[:, :, 0:HD], q_h, ACT.Copy)
                    act.activation(qe[:, :, HD:EXT], q_h[:, :, 0:FULL], ACT.Copy).then_inc(qext_done, 1)
                    act.wait_ge(kv_done, n + KV_AHEAD)
                    act.activation(kv_hi[:, u, :, :], kv[:, :, :], ACT.Copy).then_inc(kv_hi_done, 1)

        @block.gpsimd
        def _(pool):
            pool.sem_inc(toep_free, TOEP_AHEAD)
            pool.sem_inc(kv_lo_done, LO_AHEAD)
            with pool.Fori(0, H // 2) as pair:
                for u in range(2):
                    h = 2 * pair + u
                    n = h + 1
                    pool.wait_ge(toep_hi_done, n)
                    pool.tensor_tensor(toep_lo[:, u, :], toep[:, u, :], toep_hi[:, u, :].bitcast(F32), ALU.subtract)\
                        .then_inc(toep_free, 1)
                    pool.wait_ge(kv_hi_done, n)
                    pool.tensor_tensor(kv_lo[:, u, :, :], kv[:, :, :], kv_hi[:, u, :, :].bitcast(F32), ALU.subtract)\
                        .then_inc(kv_lo_done, 1)

        @block.tensor
        def _(pe):
            pe.sem_inc(y_done, Y_AHEAD)
            with pe.Fori(0, H // 2) as pair:
                for u in range(2):
                    h = 2 * pair + u
                    n = h + 1
                    pe.wait_ge(toep_free, n + TOEP_AHEAD)
                    pe.wait_ge(kv_lo_done, n + LO_AHEAD)
                    for lb in range(LB):
                        pe.wait_ge(prods_done, LB * h + lb + 2)
                        for half in range(2):
                            out = ps[lb][:, half, 0:HB * NP]
                            for ib in range(lb + 1):
                                t = slice((lb - ib) * P, (lb - ib + 1) * P)
                                r = slice(ib * B + half * HB, ib * B + (half + 1) * HB)
                                for k, (w, m) in enumerate(((toep_hi, kv_hi), (toep_hi, kv_lo), (toep_lo, kv_hi))):
                                    mm = pe.matmul(out, w[:, u, t], m[:, u, r, :].rearrange("p b n -> p (b n)"),
                                                   start=(ib == 0 and k == 0), stop=(ib == lb and k == 2))
                        mm.then_inc(y_done, 1)

        @block.vector
        def _(dve):
            dve.sem_inc(kv_done, KV_AHEAD)
            dve.sem_inc(prods_done, PRODS_AHEAD)

            def products(n, u):
                dve.wait_ge(kext_done, n)
                dve.wait_ge(kv_lo_done, n)
                ke = kext[:, u, :, :]
                k0 = ke[:, :, 0:HD]
                first = bass.AP(ke.tensor, ke.offset, [ke.ap[0], [EXT, ROWS], [0, FULL], [1, HD]])
                second = bass.AP(ke.tensor, ke.offset, [ke.ap[0], [EXT, ROWS], [1, FULL], [1, HD]])
                dve.tensor_tensor(kv[:, :, 0:FULL * HD].rearrange("p r (d j) -> p r d j", d=FULL), first, second, ALU.mult)
                dve.tensor_tensor(kv[:, :, FULL * HD:NP], k0[:, :, 0:FULL], ke[:, :, FULL:HD], ALU.mult)\
                   .then_inc(kv_done, 1)

            def weigh(h, u, lb):
                m = LB * h + lb
                v = lb % 2
                y = ps[lb][:, :, 0:HB * NP]
                q = qext[:, u, lb * B:(lb + 1) * B, :]
                pr = prods[:, v, :, :, :]
                dve.wait_ge(y_done, m + 1 + Y_AHEAD)
                part = pr.ap[0]
                yat = lambda off, dims: bass.AP(y.tensor, y.offset + off, [y.ap[0], [512, 2], [NP, HB]] + dims)
                qat = lambda off, dims: bass.AP(q.tensor, q.offset + off, [q.ap[0], [EXT * HB, 2], [EXT, HB]] + dims)
                pat = lambda off, dims: bass.AP(pr.tensor, pr.offset + off, [part, [HD * HD * HB, 2], [HD * HD, HB]] + dims)
                dve.tensor_tensor(pat(0, [[HD, FULL], [1, HD]]), yat(0, [[HD, FULL], [1, HD]]),
                                  qat(0, [[1, FULL], [1, HD]]), ALU.mult)
                dve.tensor_tensor(pat(FULL * HD + 1, [[HD + 1, FULL - 1], [1, HD]]),
                                  yat(HD, [[HD, FULL - 1], [1, HD]]),
                                  qat(0, [[0, FULL - 1], [1, HD]]), ALU.mult)
                dve.tensor_tensor(pat(FULL * HD, [[HD + 1, FULL]]), yat(FULL * HD, [[1, FULL]]),
                                  qat(FULL, [[1, FULL]]), ALU.mult)
                dve.tensor_tensor(pat(HD * HD - FULL, [[1, FULL]]), yat(FULL * HD, [[1, FULL]]),
                                  qat(0, [[1, FULL]]), ALU.mult).then_inc(prods_done, 1)
                dve.wait_ge(prods_done, m + 1 + PRODS_AHEAD)
                dve.tensor_reduce(qT[:, lb, :, bass.ds(h, 1), :].rearrange("p b h j -> p b (h j)"),
                                  pr.rearrange("p b s j -> p b j s"), AX.X, ALU.add)

            def head(h, u, last=False):
                if not last:
                    products(h + 2, 1 - u)
                dve.wait_ge(qext_done, h + 1)
                for lb in range(LB):
                    weigh(h, u, lb)

            products(1, 0)
            with dve.Fori(0, H // 2 - 1) as pair:
                for u in range(2):
                    head(2 * pair + u, u)
            head(H - 2, 0)
            head(H - 1, 1, last=True)


def run_skewed(eng, tiles, stages):
    deepest = max(lag for lag, _ in stages)
    head = deepest + deepest % 2
    for step in range(head):
        for lag, stage in stages:
            if step >= lag:
                stage((step - lag) // 2, (step - lag) % 2)
    with eng.Fori(head // 2, tiles // 2) as pair:
        for u in range(2):
            for lag, stage in stages:
                stage(pair + (u - lag) // 2, (u - lag) % 2)
    for step in range(tiles, tiles + deepest):
        for lag, stage in stages:
            if step - lag < tiles:
                stage((step - lag) // 2, (step - lag) % 2)


X_SCALE = 1024.0
PEAK = 16384.0
TINY = 1e-30


def finish_attention(nc, s, x, qT, gate_w, x2_dram, xs_dram, logits, ident):
    B, L, LB, HT, TILES, E = s["B"], s["L"], s["LB"], s["HEADS_PER_TILE"], s["TILES"], s["E"]
    with ExitStack() as c:
        sb = lambda n, sh, dt=F32: c.enter_context(nc.sbuf_tensor(n, sh, dt))
        sem = lambda n: c.enter_context(nc.semaphore(n))
        gate_sb = sb("f_gate", [P, LB, E])
        x_in = sb("f_x_in", [P, 2, L])
        sums = sb("f_sums", [P, 2, LB, P])
        x2 = sb("f_x2", [P, 2, L])
        xn = sb("f_xn", [P, 2, L])
        xs = sb("f_xs", [P, 2, 2, L], F16)
        xnT = sb("f_xnT", [P, 2, LB, P])
        stats = sb("f_stats", [P, 2, 6])
        moments = sb("f_moments", [P, 2, 2])
        var_eps = sb("f_var_eps", [P, 2, 1])
        rstd = sb("f_rstd", [P, 2, 1])
        power = sb("f_power", [P, 1])
        ps_o = [c.enter_context(nc.psum_tensor(f"f_ps_o{u}", [P, LB * P], F32)) for u in range(2)]
        ps_t = [c.enter_context(nc.psum_tensor(f"f_ps_t{u}", [P, LB * P], F32)) for u in range(2)]
        ps_l = [c.enter_context(nc.psum_tensor(f"f_ps_l{u}", [P, 512], F32)) for u in range(2)]
        gate_loaded = sem("f_gate_loaded")
        x_loaded = [sem(f"f_x_loaded{u}") for u in range(2)]
        x2_stored = [sem(f"f_x2_stored{u}") for u in range(2)]
        xs_stored = [sem(f"f_xs_stored{u}") for u in range(2)]
        picked = sem("f_picked")
        turned, x2_done, stats_done, moments_done = sem("f_turned"), sem("f_x2_done"), sem("f_stats"), sem("f_moments")
        var_eps_done, rstd_done, xn_done = sem("f_var_eps"), sem("f_rstd"), sem("f_xn_done")
        hi_done, lo_done, xn_turned, xnT_done = sem("f_hi_done"), sem("f_lo_done"), sem("f_xn_turned"), sem("f_xnT_done")
        logits_done, logits_kept = sem("f_logits_done"), sem("f_logits_kept")
        block = c.enter_context(nc.Block())

        @block.sync
        def _(sp):
            sp.dma_start(gate_sb[:, :, :], gate_w.rearrange("(a p) e -> p a e", p=P)).then_inc(gate_loaded, 16)

            def load(pair, u):
                sp.wait_ge(x2_done, 2 * pair + u + 1)
                sp.dma_start(x_in[:, u, :], x[bass.ds(pair, 1), u * P:(u + 1) * P, :]
                             .rearrange("a p l -> (a p) l")).then_inc(x_loaded[u], 16)

            def store_x2(pair, u):
                row = (2 * pair + u) * P
                sp.wait_ge(x2_done, 2 * pair + u + 3)
                sp.dma_start(x2_dram[bass.ds(row, P), :], x2[:, u, :]).then_inc(x2_stored[u], 16)

            def store_xs(pair, u):
                row = (2 * pair + u) * P
                sp.wait_ge(lo_done, 2 * pair + u + 3)
                sp.dma_start(xs_dram[bass.ds(row, P), :], xs[:, u, :, :].rearrange("p a l -> p (a l)"))\
                  .then_inc(xs_stored[u], 16)

            run_skewed(sp, TILES, [(0, load), (1, store_x2), (3, store_xs)])
            for u in range(2):
                sp.wait_ge(x2_stored[u], 16 * (B + 1))
                sp.wait_ge(xs_stored[u], 16 * (B + 1))

        @block.tensor
        def _(pe):
            def turn_sums(pair, u):
                pe.wait_ge(x2_done, 2 * pair + u + 1)
                pe.wait_ge(picked, 2 * pair + u + 1)
                for lb in range(LB):
                    mm = pe.transpose(ps_o[u][:, lb * P:(lb + 1) * P], sums[:, u, lb, :], ident[:, :])
                mm.then_inc(turned, 1)

            def turn_normed(pair, u):
                n = 2 * pair + u + 1
                pe.wait_ge(xn_done, n)
                pe.wait_ge(xnT_done, n)
                for lb in range(LB):
                    mm = pe.transpose(ps_t[u][:, lb * P:(lb + 1) * P], xn[:, u, lb * P:(lb + 1) * P], ident[:, :])
                mm.then_inc(xn_turned, 1)

            def route_logits(pair, u):
                n = 2 * pair + u + 1
                pe.wait_ge(xnT_done, n + 2)
                pe.wait_ge(logits_kept, n)
                for lb in range(LB):
                    mm = pe.matmul(ps_l[u][:, 0:E], xnT[:, u, lb, :], gate_sb[:, lb, :], start=(lb == 0), stop=(lb == LB - 1))
                mm.then_inc(logits_done, 1)

            pe.wait_ge(gate_loaded, 16)
            pe.sem_inc(turned, 2)
            pe.sem_inc(logits_done, 2)
            run_skewed(pe, TILES, [(0, turn_sums), (2, turn_normed), (3, route_logits)])

        @block.vector
        def _(dve):
            def add(pair, u):
                n = 2 * pair + u + 1
                dve.wait_ge(turned, n + 2)
                dve.wait_ge(x_loaded[u], 16 * pair + 16)
                dve.wait_ge(x2_stored[u], 16 * pair + 16)
                dve.tensor_tensor(x2[:, u, :], ps_o[u][:, :], x_in[:, u, :], ALU.add).then_inc(x2_done, 1)
                dve.wait_ge(x2_done, n + 2)
                dve.bn_stats(stats[:, u, :], x2[:, u, :]).then_inc(stats_done, 1)
                dve.wait_ge(stats_done, n)
                pass_waits(dve, s)
                dve.bn_aggr(moments[:, u, :], stats[:, u, :]).then_inc(moments_done, 1)

            def normalise(pair, u):
                n = 2 * pair + u + 1
                dve.wait_ge(rstd_done, n)
                dve.wait_ge(xnT_done, n)
                dve.wait_ge(lo_done, n)
                dve.tensor_scalar(xn[:, u, :], x2[:, u, :], moments[:, u, 0:1], rstd[:, u, :],
                                  ALU.subtract, ALU.mult).then_inc(xn_done, 1)

            def split(pair, u):
                n = 2 * pair + u + 1
                dve.wait_ge(hi_done, n)
                dve.scalar_tensor_tensor(xs[:, u, 1, :], xn[:, u, :], X_SCALE, xs[:, u, 0, :], ALU.mult,
                                         ALU.subtract).then_inc(lo_done, 1)

            def keep_logits(pair, u):
                n = 2 * pair + u + 1
                dve.wait_ge(logits_done, n + 2)
                dve.tensor_copy(logits[:, bass.ds(2 * pair + u, 1), :].rearrange("p a e -> p (a e)"), ps_l[u][:, 0:E])\
                   .then_inc(logits_kept, 1)

            dve.sem_inc(x2_done, 2)
            dve.sem_inc(lo_done, 2)
            dve.sem_inc(logits_kept, 2)
            run_skewed(dve, TILES, [(0, add), (1, normalise), (2, split), (5, keep_logits)])

        @block.gpsimd
        def _(pool):
            for u in range(2):
                pool.sem_inc(x2_stored[u], 16)
                pool.sem_inc(xs_stored[u], 16)
            pool.memset(power[:, :], -0.5).then_inc(var_eps_done, 1)
            with pool.Fori(0, B) as b:
                for u in range(2):
                    n = 2 * b + u + 1
                    pool.wait_ge(moments_done, n)
                    pass_waits(pool, s)
                    pool.tensor_scalar(var_eps[:, u, :], moments[:, u, 1:2], EPS, None, ALU.add)\
                        .then_inc(var_eps_done, 1)
                    pool.wait_ge(var_eps_done, n + 1)
                    pool.tensor_tensor(rstd[:, u, :], var_eps[:, u, :], power[:, :], ALU.pow)\
                        .then_inc(rstd_done, 1)

        @block.scalar
        def _(act):
            def pick(pair, u):
                act.wait_ge(turned, 2 * pair + u + 1)
                act.activation(sums[:, u, :, :], qT[:, :, bass.ds(pair, 1), u * HT:(u + 1) * HT, :]
                               .rearrange("p a b h j -> p a (b h j)"), ACT.Copy).then_inc(picked, 1)

            def high(pair, u):
                n = 2 * pair + u + 1
                act.wait_ge(xn_done, n)
                act.wait_ge(xs_stored[u], 16 * pair + 16)
                act.activation(xs[:, u, 0, :], xn[:, u, :], ACT.Copy, scale=X_SCALE).then_inc(hi_done, 1)

            def keep_turned(pair, u):
                n = 2 * pair + u + 1
                act.wait_ge(xn_turned, n)
                act.wait_ge(logits_done, n)
                act.activation(xnT[:, u, :, :].rearrange("p a t -> p (a t)"), ps_t[u][:, :], ACT.Copy).then_inc(xnT_done, 1)

            act.sem_inc(xnT_done, 2)
            run_skewed(act, TILES, [(0, pick), (3, keep_turned), (1, high)])


def fill_sorted(nc, s, xsort):
    with ExitStack() as c:
        zero = c.enter_context(nc.sbuf_tensor("zero_rows", [P, 2 * s["L"]], F16))
        zeroed, filled = c.enter_context(nc.semaphore("zero_zeroed")), c.enter_context(nc.semaphore("sorted_filled"))
        block = c.enter_context(nc.Block())

        @block.gpsimd
        def _(pool):
            pool.memset(zero[:, :], 0.0).then_inc(zeroed, 1)

        @block.sync
        def _(sp):
            sp.wait_ge(zeroed, 1)
            with sp.Fori(0, s["SORTED_TILES"]) as i:
                sp.dma_start(xsort[bass.ds(i * P, P), :], zero[:, :]).then_inc(filled, 16)
            sp.wait_ge(filled, 16 * s["SORTED_TILES"])


def split_weights(nc, s, w, gu_hi, gu_lo, down_hi, down_lo, scales):
    LB, F, L, E, FB = s["LB"], s["F"], s["L"], s["E"], s["FB"]
    LAST = F - (FB - 1) * P
    with ExitStack() as c:
        sb = lambda n, sh, dt=F32: c.enter_context(nc.sbuf_tensor(n, sh, dt))
        sem = lambda n: c.enter_context(nc.semaphore(n))
        gu = sb("w_gu", [P, LB, 2 * F])
        down = sb("w_down", [P, FB, L])
        peaks = sb("w_peaks", [P, 4])
        peak = sb("w_peak", [P, 4])
        inv = sb("w_inv", [P, 3])
        scale = sb("w_scale", [P, 3])
        loaded, peaks_done, peak_done, chain = sem("w_loaded"), sem("w_peaks"), sem("w_peak"), sem("w_chain")
        scale_done, hi_done, lo_done, cleared = sem("w_scale_done"), sem("w_hi_done"), sem("w_lo_done"), sem("w_cleared")
        block = c.enter_context(nc.Block())
        SHARED = [(h * F, (h + 1) * F) for h in range(2)]

        def over_experts(eng, one):
            with eng.Fori(0, E) as e:
                one(e, None)
            for h in range(2):
                one(E + h, h)

        @block.sync
        def _(sp):
            def one(e, half):
                sp.wait_ge(lo_done, e + 1)
                if half is None:
                    wg, wu = (w[k][bass.ds(e, 1), :, :].rearrange("a (c p) f -> p (a c) f", p=P) for k in ("gate", "up"))
                    wd = w["down"][bass.ds(e, 1), :, :].rearrange("a f l -> (a f) l")
                else:
                    at = slice(half * F, (half + 1) * F)
                    wg, wu = (w[k][:, at].rearrange("(c p) f -> p c f", p=P) for k in ("s_gate", "s_up"))
                    wd = w["s_down"][at, :]
                sp.dma_start(gu[:, :, 0:F], wg).then_inc(loaded, 16)
                sp.dma_start(gu[:, :, F:2 * F], wu).then_inc(loaded, 16)
                sp.dma_start(down[:, 0:FB - 1, :], wd[0:(FB - 1) * P, :].rearrange("(c p) l -> p c l", p=P)).then_inc(loaded, 16)
                sp.dma_start(down[0:LAST, FB - 1, :], wd[(FB - 1) * P:F, :]).then_inc(loaded, 16)

            over_experts(sp, one)

        @block.gpsimd
        def _(pool):
            def one(e, half):
                pool.wait_ge(peaks_done, e + 1)
                pass_waits(pool, s)
                pool.partition_all_reduce(peak[:, :], peaks[:, :], P, bass.bass_isa.ReduceOp.max).then_inc(peak_done, 1)

            over_experts(pool, one)

        @block.scalar
        def _(act):
            def one(e, half):
                act.wait_ge(scale_done, e + 1)
                for k, at in enumerate((slice(0, F), slice(F, 2 * F))):
                    act.activation(gu_hi[:, bass.ds(e, 1), :, at].rearrange("p a c f -> p (a c) f"), gu[:, :, at], ACT.Copy,
                                   scale=scale[:, k:k + 1])
                act.activation(down_hi[:, bass.ds(e, 1), 0:FB - 1, :].rearrange("p a c f -> p (a c) f"),
                               down[:, 0:FB - 1, :], ACT.Copy, scale=scale[:, 2:3])
                act.activation(down_hi[0:LAST, bass.ds(e, 1), FB - 1, :].rearrange("p a f -> p (a f)"),
                               down[0:LAST, FB - 1, :], ACT.Copy, scale=scale[0:LAST, 2:3]).then_inc(hi_done, 1)

            over_experts(act, one)

        @block.vector
        def _(dve):
            STEPS = 2
            dve.memset(peaks[:, 3:4], 0.0).then_inc(cleared, 1)
            dve.sem_inc(lo_done, 1)
            dve.wait_ge(cleared, 1)

            def one(e, half):
                dve.wait_ge(loaded, 64 * e + 64)
                for k, at in enumerate((slice(0, F), slice(F, 2 * F))):
                    dve.tensor_reduce(peaks[:, k:k + 1], gu[:, :, at], AX.XY, ALU.max, apply_absolute_value=True)
                dve.tensor_reduce(peaks[:, 2:3], down[:, 0:FB - 1, :], AX.XY, ALU.max, apply_absolute_value=True)
                dve.tensor_reduce(peaks[0:LAST, 3:4], down[0:LAST, FB - 1, :], AX.X, ALU.max,
                                  apply_absolute_value=True).then_inc(peaks_done, 1)
                dve.wait_ge(peak_done, e + 1)
                dve.tensor_tensor(peak[:, 2:3], peak[:, 2:3], peak[:, 3:4], ALU.max).then_inc(chain, 1)
                dve.wait_ge(chain, STEPS * e + 1)
                dve.tensor_scalar(inv[:, :], peak[:, 0:3], TINY, 1.0 / PEAK, ALU.max, ALU.mult).then_inc(chain, 1)
                dve.wait_ge(chain, STEPS * e + 2)
                sc = scales[:, bass.ds(e, 1), :].rearrange("p a k -> p (a k)")
                dve.tensor_scalar(sc[:, 0:2], inv[:, 0:2], 1.0 / X_SCALE, None, ALU.mult)
                dve.tensor_copy(sc[:, 2:3], inv[:, 2:3])
                dve.reciprocal(scale[:, :], inv[:, :]).then_inc(scale_done, 1)
                dve.wait_ge(hi_done, e + 1)
                for k, at in enumerate((slice(0, F), slice(F, 2 * F))):
                    dve.scalar_tensor_tensor(gu_lo[:, bass.ds(e, 1), :, at].rearrange("p a c f -> p (a c) f"), gu[:, :, at],
                                             scale[:, k:k + 1],
                                             gu_hi[:, bass.ds(e, 1), :, at].rearrange("p a c f -> p (a c) f"),
                                             ALU.mult, ALU.subtract)
                dve.scalar_tensor_tensor(down_lo[:, bass.ds(e, 1), 0:FB - 1, :].rearrange("p a c f -> p (a c) f"),
                                         down[:, 0:FB - 1, :], scale[:, 2:3],
                                         down_hi[:, bass.ds(e, 1), 0:FB - 1, :].rearrange("p a c f -> p (a c) f"),
                                         ALU.mult, ALU.subtract)
                dve.scalar_tensor_tensor(down_lo[0:LAST, bass.ds(e, 1), FB - 1, :].rearrange("p a f -> p (a f)"),
                                         down[0:LAST, FB - 1, :], scale[0:LAST, 2:3],
                                         down_hi[0:LAST, bass.ds(e, 1), FB - 1, :].rearrange("p a f -> p (a f)"),
                                         ALU.mult, ALU.subtract).then_inc(lo_done, 1)

            over_experts(dve, one)


def route(nc, s, logits, slots, tops, tile_expert, ident):
    TILES, E, NT = s["TILES"], s["E"], s["SORTED_TILES"]
    N = TILES * E
    with ExitStack() as c:
        sb = lambda n, sh, dt=F32: c.enter_context(nc.sbuf_tensor(n, sh, dt))
        sem = lambda n: c.enter_context(nc.semaphore(n))
        top = sb("r_top", [P, TILES])
        shifted = sb("r_shifted", [P, TILES, E])
        scores = sb("r_scores", [P, TILES, E])
        rest = sb("r_rest", [P, TILES, E])
        equal = sb("r_equal", [P, TILES, E])
        first = sb("r_first", [P, TILES])
        chosen = sb("r_chosen", [P, 2, TILES, E])
        mask = sb("r_mask", [P, TILES, E])
        expert_no = sb("r_expert_no", [P, E])
        before = sb("r_before", [P, P])
        ones = sb("r_ones", [P, P])
        goes_on = sb("r_goes_on", [P, E, TILES])
        totals = sb("r_totals", [P, E, TILES])
        sums = sb("r_sums", [P, E, TILES])
        starts = sb("r_starts", [P, TILES])
        full = sb("r_full", [P, E, TILES])
        tiles_of = sb("r_tiles_of", [P, E])
        ends = sb("r_ends", [P, E])
        base = sb("r_base", [P, E])
        row = sb("r_row", [P, TILES, E])
        picked = sb("r_picked", [P, TILES, E])
        slot_f = sb("r_slot_f", [P, 2, TILES])
        tile_no = sb("r_tile_no", [P, NT])
        passed = sb("r_passed", [P, NT, E - 1])
        passed_n = sb("r_passed_n", [P, NT])
        ps = c.enter_context(nc.psum_tensor("r_ps", [P, 2, 512], F32))
        drawn, exp_done, exp_ready, step = sem("r_drawn"), sem("r_exp_done"), sem("r_exp_ready"), sem("r_step")
        mask_ready, counted = sem("r_mask_ready"), sem("r_counted")
        block = c.enter_context(nc.Block())

        @block.gpsimd
        def _(pool):
            kw = dict(allow_small_or_imprecise_dtypes=True)
            pool.iota(expert_no[:, :], [[1, E]], base=0, channel_multiplier=0, **kw).then_inc(drawn, 1)
            pool.iota(starts[:, :], [[P, TILES]], base=0, channel_multiplier=0, **kw).then_inc(drawn, 1)
            pool.iota(tile_no[:, :], [[1, NT]], base=0, channel_multiplier=0, **kw).then_inc(drawn, 1)
            pool.memset(ones[:, :], 1.0).then_inc(drawn, 1)
            pool.memset(goes_on[:, :, :], 1.0).then_inc(drawn, 1)
            pool.wait_ge(drawn, 5)
            pool.affine_select(out=before[:, :], in_=ones[:, :], compare_op=ALU.is_gt, fill=0.0, base=0,
                               pattern=[[1, P]], channel_multiplier=-1).then_inc(drawn, 1)
            pool.memset(goes_on[:, :, 0:1], 0.0).then_inc(drawn, 1)

        @block.scalar
        def _(act):
            act.wait_ge(exp_ready, 1)
            act.activation(scores[:, :, :], shifted[:, :, :], ACT.Exp).then_inc(exp_done, 1)

        @block.tensor
        def _(pe):
            pe.wait_ge(mask_ready, 1)
            m = mask[:, :, :].rearrange("p t e -> p (t e)")
            pe.matmul(ps[:, 0, 0:N], before[:, :], m, start=True, stop=True)
            pe.matmul(ps[:, 1, 0:N], ones[:, :], m, start=True, stop=True).then_inc(counted, 1)

        @block.vector
        def _(dve):
            done = [0]

            def then(ins):
                done[0] += 1
                ins.then_inc(step, 1)
                dve.wait_ge(step, done[0])


            each = lambda a: bass.AP(a.tensor, a.offset, [a.ap[0], [1, TILES], [0, E]])
            all_tiles = lambda a: bass.AP(a.tensor, a.offset, [a.ap[0], [0, TILES], [1, E]])
            then(dve.tensor_reduce(top[:, :], logits[:, :, :], AX.X, ALU.max))
            dve.tensor_tensor(shifted[:, :, :], logits[:, :, :], each(top[:, :]), ALU.subtract).then_inc(exp_ready, 1)
            dve.wait_ge(exp_done, 1)
            then(dve.tensor_reduce(top[:, :], scores[:, :, :], AX.X, ALU.add))
            then(dve.reciprocal(first[:, :], top[:, :]))
            then(dve.tensor_tensor(rest[:, :, :], scores[:, :, :], each(first[:, :]), ALU.mult))
            dve.wait_ge(drawn, 7)
            for k in range(2):
                then(dve.tensor_reduce(tops[:, k, :], rest[:, :, :], AX.X, ALU.max))
                then(dve.tensor_tensor(equal[:, :, :], rest[:, :, :], each(tops[:, k, :]), ALU.is_equal))
                then(dve.tensor_scalar(equal[:, :, :], equal[:, :, :], -float(E), float(E), ALU.mult, ALU.add))
                then(dve.tensor_tensor(equal[:, :, :], equal[:, :, :], all_tiles(expert_no[:, :]), ALU.add))
                then(dve.tensor_reduce(first[:, :], equal[:, :, :], AX.X, ALU.min))
                then(dve.tensor_tensor(chosen[:, k, :, :], all_tiles(expert_no[:, :]), each(first[:, :]), ALU.is_equal))
                if k == 0:
                    then(dve.scalar_tensor_tensor(rest[:, :, :], chosen[:, k, :, :], -4.0, rest[:, :, :], ALU.mult, ALU.add))
            dve.tensor_tensor(mask[:, :, :], chosen[:, 0, :, :], chosen[:, 1, :, :], ALU.add).then_inc(mask_ready, 1)
            dve.wait_ge(counted, 1)
            then(dve.tensor_copy(totals[:, :, :], ps[:, 1, 0:N].rearrange("p (t e) -> p e t", e=E)))
            flat = lambda a: a.rearrange("p e t -> p (e t)")
            then(dve.tensor_tensor_scan(flat(sums[:, :, :]), flat(goes_on[:, :, :]), flat(totals[:, :, :]), 0.0,
                                        ALU.mult, ALU.add))
            count = sums[:, :, TILES - 1:TILES]
            then(dve.tensor_tensor(full[:, :, :], bass.AP(count.tensor, count.offset, [count.ap[0], [TILES, E], [0, TILES]]),
                                   bass.AP(starts, 0, [starts[:, :].ap[0], [0, E], [1, TILES]]), ALU.is_gt))
            then(dve.tensor_reduce(tiles_of[:, :], full[:, :, :], AX.X, ALU.add))
            then(dve.tensor_tensor_scan(ends[:, :], ones[:, 0:E], tiles_of[:, :], 0.0, ALU.mult, ALU.add))
            then(dve.tensor_tensor(base[:, :], ends[:, :], tiles_of[:, :], ALU.subtract))
            then(dve.tensor_tensor(sums[:, :, :], sums[:, :, :], totals[:, :, :], ALU.subtract))
            then(dve.scalar_tensor_tensor(row[:, :, :], all_tiles(base[:, :]), float(P),
                                          sums[:, :, :].rearrange("p e t -> p t e"), ALU.mult, ALU.add))
            then(dve.tensor_tensor(row[:, :, :], row[:, :, :], ps[:, 0, 0:N].rearrange("p (t e) -> p t e", e=E), ALU.add))
            for k in range(2):
                then(dve.tensor_tensor(picked[:, :, :], chosen[:, k, :, :], row[:, :, :], ALU.mult))
                then(dve.tensor_reduce(slot_f[:, k, :], picked[:, :, :], AX.X, ALU.add))
            dve.tensor_copy(slots[:, :, :], slot_f[:, :, :])
            then(dve.tensor_tensor(passed[:, :, :], bass.AP(tile_no, 0, [tile_no[:, :].ap[0], [1, NT], [0, E - 1]]),
                                   bass.AP(ends, 0, [ends[:, :].ap[0], [0, NT], [1, E - 1]]), ALU.is_ge))
            then(dve.tensor_reduce(passed_n[:, :], passed[:, :, :], AX.X, ALU.add))
            then(dve.tensor_copy(tile_expert[:, :], passed_n[:, :]))


def scatter_tokens(nc, s, xs_dram, xsort, slots):
    TILES, L, B = s["TILES"], s["L"], s["B"]
    with ExitStack() as c:
        xs = c.enter_context(nc.sbuf_tensor("t_xs", [P, 4, 2 * L], F16))
        loaded = [c.enter_context(nc.semaphore(f"t_loaded{u}")) for u in range(4)]
        sent = [c.enter_context(nc.semaphore(f"t_sent{u}")) for u in range(4)]
        block = c.enter_context(nc.Block())

        @block.sync
        def _(sp):
            for u in range(4):
                sp.dma_start(xs[:, u, :], xs_dram[u * P:(u + 1) * P, :]).then_inc(loaded[u], 16)
            with sp.Fori(1, TILES // 4) as i:
                for u in range(4):
                    sp.wait_ge(sent[u], 32 * i)
                    sp.dma_start(xs[:, u, :], xs_dram[bass.ds((4 * i + u) * P, P), :]).then_inc(loaded[u], 16)

        @block.gpsimd
        def _(pool):
            for t in range(TILES):
                u = t % 4
                pool.wait_ge(loaded[u], 16 * (t // 4 + 1))
                for k in range(2):
                    pool.indirect_dma_start(out=xsort[:, :], out_offset=bass.IndirectOffsetOnAxis(ap=slots[:, k, t:t + 1], axis=0),
                                            in_=xs[:, u, :], in_offset=None).then_inc(sent[u], 16)
            for u in range(4):
                pool.wait_ge(sent[u], 32 * (TILES // 4))


def expert_tiles(nc, s, tiles, x_rows, expert_of, weights, scales, ident16, y_dram=None, x2_dram=None, tag=""):
    LB, F, L, FB = s["LB"], s["F"], s["L"], s["FB"]
    LAST = F - (FB - 1) * P
    gu_hi, gu_lo, down_hi, down_lo = weights
    shared = x2_dram is not None
    with ExitStack() as c:
        sb = lambda n, sh, dt=F32: c.enter_context(nc.sbuf_tensor(tag + n, sh, dt))
        psum = lambda n, sh, dt=F32: c.enter_context(nc.psum_tensor(tag + n, sh, dt))
        sem = lambda n: c.enter_context(nc.semaphore(tag + n))
        xs = sb("xs", [P, 2, 2 * LB, P], F16)
        xT = sb("xT", [P, 2, 2 * LB, P], F16)
        gated = sb("gated", [P, 2, F])
        hid = sb("hid", [P, 2, F])
        hpeak, hinv, hscale, yscale = (sb(n, [P, 2, 1]) for n in ("hpeak", "hinv", "hscale", "yscale"))
        h16 = sb("h16", [P, 2, 2, F], F16)
        hT = sb("hT", [P, 2, 2, FB, P], F16)
        y = sb("y", [P, 2, L])
        ps_gu = [psum(f"ps_gu{u}", [P, 2, 512]) for u in range(2)]
        ps_x = psum("ps_x", [P, 2 * LB, P], F16)
        ps_h = psum("ps_h", [P, 2, FB, P], F16)
        ps_y = psum("ps_y", [P, 2, 512])
        loaded = [sem(f"loaded{u}") for u in range(2)]
        stored = [sem(f"stored{u}") for u in range(2)]
        x_turned, xT_done, gate_done, up_done = sem("x_turned"), sem("xT_done"), sem("gate_done"), sem("up_done")
        gated_done, hid_done, small, h_hi_done, h_lo_done = (sem(n) for n in ("gated_done", "hid_done", "small", "h_hi", "h_lo"))
        yscale_done = sem("yscale_done")
        h_turned, hT_done, down_done, y_done = sem("h_turned"), sem("hT_done"), sem("down_done"), sem("y_done")
        if shared:
            x2 = sb("x2", [P, 2, L])
            x2_loaded = [sem(f"x2_loaded{u}") for u in range(2)]
        block = c.enter_context(nc.Block())
        no = lambda pair, u: 2 * pair + u + 1

        @block.sync
        def _(sp):
            def load(pair, u):
                sp.wait_ge(x_turned, no(pair, u))
                sp.dma_start(xs[:, u, :, :].rearrange("p a t -> p (a t)"), x_rows(pair, u)).then_inc(loaded[u], 16)
                if shared and u == 0:
                    pass

            def load_x2(pair, u):
                if shared and u == 0:
                    sp.wait_ge(y_done, 2 * pair + 1)
                    sp.dma_start(x2[:, 0, :], x2_dram[bass.ds(pair * P, P), :]).then_inc(x2_loaded[0], 16)

            def store(pair, u):
                sp.wait_ge(y_done, no(pair, u) + 2)
                pass_waits(sp, s)
                if not shared:
                    sp.dma_start(y_dram[bass.ds((2 * pair + u) * P, P), :], y[:, u, :]).then_inc(stored[u], 16)
                elif u == 1:
                    sp.dma_start(x2_dram[bass.ds(pair * P, P), :], y[:, 1, :]).then_inc(stored[u], 16)

            for u in range(2):
                sp.sem_inc(stored[u], 16)
            run_skewed(sp, tiles, [(0, load), (1, load_x2), (4, store)])
            for u in range(2):
                if not shared or u == 1:
                    sp.wait_ge(stored[u], 16 * (tiles // 2) + 16)

        @block.tensor
        def _(pe):
            experts = {}

            def turn_x(pair, u):
                pe.wait_ge(loaded[u], 16 * pair + 16)
                pe.wait_ge(xT_done, no(pair, u) + 1)
                for n in range(2 * LB):
                    mm = pe.transpose(ps_x[:, n, :], xs[:, u, n, :], ident16[:, :])
                mm.then_inc(x_turned, 1)

            def project(pair, u, k, ready, done):
                e = experts[u]
                out = ps_gu[u][:, k, 0:F]
                for kb in range(LB):
                    for n, (a, b) in enumerate(((0, gu_hi), (0, gu_lo), (1, gu_hi))):
                        mm = pe.matmul(out, xT[:, u, a * LB + kb, :],
                                       b[:, bass.ds(e, 1), kb, k * F:(k + 1) * F].rearrange("p a f -> p (a f)"),
                                       start=(kb == 0 and n == 0), stop=(kb == LB - 1 and n == 2))
                mm.then_inc(done, 1)

            def gate(pair, u):
                experts[u] = expert_of(pe, pair, u)
                pe.wait_ge(xT_done, no(pair, u) + 2)
                pe.wait_ge(hid_done, no(pair, u))
                project(pair, u, 0, None, gate_done)

            def up(pair, u):
                project(pair, u, 1, None, up_done)

            def turn_h(pair, u):
                pe.wait_ge(h_lo_done, no(pair, u))
                pe.wait_ge(hT_done, no(pair, u) + 1)
                for part in range(2):
                    for fb in range(FB):
                        rows = P if fb < FB - 1 else LAST
                        mm = pe.transpose(ps_h[0:rows, part, fb, :], h16[:, u, part, fb * P:fb * P + rows], ident16[:, :])
                mm.then_inc(h_turned, 1)

            def down(pair, u):
                e = down_expert[u]
                pe.wait_ge(hT_done, no(pair, u) + 2)
                pe.wait_ge(y_done, no(pair, u))
                for fb in range(FB):
                    rows = P if fb < FB - 1 else LAST
                    for n, (a, b) in enumerate(((0, down_hi), (0, down_lo), (1, down_hi))):
                        mm = pe.matmul(ps_y[:, u, :], hT[0:rows, u, a, fb, :],
                                       b[0:rows, bass.ds(e, 1), fb, :].rearrange("p a f -> p (a f)"),
                                       start=(fb == 0 and n == 0), stop=(fb == FB - 1 and n == 2))
                mm.then_inc(down_done, 1)

            down_expert = {}

            def pick_down(pair, u):
                down_expert[u] = expert_of(pe, pair, u)

            pe.sem_inc(x_turned, 2)
            run_skewed(pe, tiles, [(0, turn_x), (1, gate), (2, turn_h), (1, up), (2, pick_down), (2, down)])

        @block.scalar
        def _(act):
            def swish(pair, u):
                e = expert_of(act, pair, u)
                act.wait_ge(gate_done, no(pair, u))
                act.wait_ge(hid_done, no(pair, u))
                act.activation(gated[:, u, :], ps_gu[u][:, 0, 0:F], ACT.Silu,
                               scale=scales[:, bass.ds(e, 1), 0:1].rearrange("p a k -> p (a k)")).then_inc(gated_done, 1)

            def high(pair, u):
                act.wait_ge(small, 3 * no(pair, u))
                act.wait_ge(h_turned, no(pair, u))
                act.activation(h16[:, u, 0, :], hid[:, u, :], ACT.Copy, scale=hscale[:, u, :]).then_inc(h_hi_done, 1)

            def keep_hT(pair, u):
                act.wait_ge(h_turned, no(pair, u) + 2)
                act.wait_ge(down_done, no(pair, u))
                act.activation(hT[:, u, :, 0:FB - 1, :], ps_h[:, :, 0:FB - 1, :], ACT.Copy)
                act.activation(hT[0:LAST, u, :, FB - 1, :], ps_h[0:LAST, :, FB - 1, :], ACT.Copy).then_inc(hT_done, 1)

            def result(pair, u):
                if shared:
                    return
                act.wait_ge(down_done, no(pair, u) + 2)
                act.wait_ge(yscale_done, no(pair, u))
                act.wait_ge(stored[u], 16 * pair + 16)
                act.activation(y[:, u, :], ps_y[:, u, :], ACT.Copy, scale=yscale[:, u, :]).then_inc(y_done, 1)

            act.sem_inc(hT_done, 2)
            if not shared:
                act.sem_inc(y_done, 2)
            run_skewed(act, tiles, [(1, keep_hT), (0, swish), (0, high), (1, result)])

        @block.vector
        def _(dve):
            def keep_xT(pair, u):
                dve.wait_ge(x_turned, no(pair, u) + 2)
                dve.wait_ge(up_done, no(pair, u))
                dve.tensor_copy(xT[:, u, :, :], ps_x[:, :, :]).then_inc(xT_done, 1)

            def hidden(pair, u):
                e = expert_of(dve, pair, u)
                n = no(pair, u)
                dve.wait_ge(up_done, n + 2)
                dve.wait_ge(gated_done, n)
                dve.scalar_tensor_tensor(hid[:, u, :], ps_gu[u][:, 1, 0:F],
                                         scales[:, bass.ds(e, 1), 1:2].rearrange("p a k -> p (a k)"),
                                         gated[:, u, :], ALU.mult, ALU.mult).then_inc(hid_done, 1)
                dve.wait_ge(hid_done, n + 2)
                dve.tensor_reduce(hpeak[:, u, :], hid[:, u, :], AX.X, ALU.max, apply_absolute_value=True).then_inc(small, 1)
                dve.wait_ge(small, 3 * n - 2)
                dve.tensor_scalar(hinv[:, u, :], hpeak[:, u, :], TINY, 1.0 / PEAK, ALU.max, ALU.mult).then_inc(small, 1)
                dve.wait_ge(small, 3 * n - 1)
                dve.reciprocal(hscale[:, u, :], hinv[:, u, :]).then_inc(small, 1)
                dve.wait_ge(y_done, n)
                dve.tensor_tensor(yscale[:, u, :], hinv[:, u, :],
                                  scales[:, bass.ds(e, 1), 2:3].rearrange("p a k -> p (a k)"), ALU.mult)\
                   .then_inc(yscale_done, 1)
                dve.wait_ge(h_hi_done, n)
                dve.scalar_tensor_tensor(h16[:, u, 1, :], hid[:, u, :], hscale[:, u, :], h16[:, u, 0, :], ALU.mult,
                                         ALU.subtract).then_inc(h_lo_done, 1)

            def result(pair, u):
                if not shared:
                    return
                n = no(pair, u)
                dve.wait_ge(down_done, n + 2)
                dve.wait_ge(yscale_done, n)
                if u == 0:
                    dve.wait_ge(x2_loaded[0], 16 * pair + 16)
                    dve.wait_ge(y_done, n + 1)
                    src = x2[:, 0, :]
                else:
                    dve.wait_ge(y_done, n + 1)
                    dve.wait_ge(stored[1], 16 * pair + 16)
                    src = y[:, 0, :]
                dve.scalar_tensor_tensor(y[:, u, :], ps_y[:, u, :], yscale[:, u, :], src, ALU.mult, ALU.add)\
                   .then_inc(y_done, 1)

            dve.sem_inc(xT_done, 2)
            dve.sem_inc(up_done, 2)
            dve.sem_inc(hid_done, 2)
            dve.sem_inc(h_turned, 2)
            dve.sem_inc(down_done, 2)
            if shared:
                dve.sem_inc(y_done, 2)
            run_skewed(dve, tiles, [(0, keep_xT), (1, hidden), (2, result)])


def combine(nc, s, r_dram, y_dram, slots, tops, out):
    TILES, L = s["TILES"], s["L"]
    SL = 4
    with ExitStack() as c:
        sb = lambda n, sh, dt=F32: c.enter_context(nc.sbuf_tensor("c_" + n, sh, dt))
        sem = lambda n: c.enter_context(nc.semaphore("c_" + n))
        r = sb("r", [P, SL, L])
        g = sb("g", [P, SL, 2, L])
        acc = sb("acc", [P, SL, L])
        o = sb("o", [P, SL, L])
        r_loaded, g_loaded, stored = ([sem(f"{n}{u}") for u in range(SL)] for n in ("r_loaded", "g_loaded", "stored"))
        first_done, out_done = sem("first_done"), sem("out_done")
        block = c.enter_context(nc.Block())
        rows = lambda a, t: a[t * P:(t + 1) * P, :]
        out_rows = out.rearrange("b c l -> (b c) l")

        @block.sync
        def _(sp):
            for t in range(TILES + 2):
                if t < TILES:
                    if t >= SL:
                        sp.wait_ge(first_done, t - SL + 1)
                    sp.dma_start(r[:, t % SL, :], rows(r_dram, t)).then_inc(r_loaded[t % SL], 16)
                if t >= 2:
                    sp.wait_ge(out_done, t - 1)
                    sp.dma_start(rows(out_rows, t - 2), o[:, (t - 2) % SL, :]).then_inc(stored[(t - 2) % SL], 16)
            for u in range(SL):
                sp.wait_ge(stored[u], 16 * (TILES // SL))

        @block.gpsimd
        def _(pool):
            for t in range(TILES):
                if t >= SL:
                    pool.wait_ge(out_done, t - SL + 1)
                for k in range(2):
                    pool.indirect_dma_start(out=g[:, t % SL, k, :], out_offset=None, in_=y_dram[:, :],
                                            in_offset=bass.IndirectOffsetOnAxis(ap=slots[:, k, t:t + 1], axis=0))\
                        .then_inc(g_loaded[t % SL], 16)

        @block.vector
        def _(dve):
            for t in range(TILES):
                u = t % SL
                dve.wait_ge(r_loaded[u], 16 * (t // SL + 1))
                dve.wait_ge(g_loaded[u], 32 * (t // SL + 1))
                dve.scalar_tensor_tensor(acc[:, u, :], g[:, u, 0, :], tops[:, 0, t:t + 1], r[:, u, :], ALU.mult, ALU.add)\
                   .then_inc(first_done, 1)
                dve.wait_ge(first_done, t + 1)
                if t >= SL:
                    dve.wait_ge(stored[u], 16 * (t // SL))
                dve.scalar_tensor_tensor(o[:, u, :], g[:, u, 1, :], tops[:, 1, t:t + 1], acc[:, u, :], ALU.mult, ALU.add)\
                   .then_inc(out_done, 1)


def build(nc, x, ctx_in, ssm_kernel, dvec, gate_w, w_gate, w_up, w_down, sw_gate, sw_up, sw_down, out):
    s = shapes_of(x, ssm_kernel, gate_w, w_gate)
    B, L, LB, H, HD, E, F, TILES = (s[k] for k in ("B", "L", "LB", "H", "HD", "E", "F", "TILES"))
    s["FB"] = -(-F // P)
    s["SORTED_TILES"] = 2 * TILES + E
    w = {"gate": w_gate, "up": w_up, "down": w_down, "s_gate": sw_gate, "s_up": sw_up, "s_down": sw_down}
    kpad = nc.dram_tensor("kpad", [H, P + L], F32)
    x2_dram = nc.dram_tensor("x2_rows", [s["TOKENS"], L], F32)
    xs_dram = nc.dram_tensor("xs_rows", [s["TOKENS"], 2 * L], F16)
    xsort = nc.dram_tensor("x_sorted", [s["SORTED_TILES"] * P, 2 * L], F16)
    y_dram = nc.dram_tensor("y_sorted", [s["SORTED_TILES"] * P, L], F32)
    with ExitStack() as c:
        sb = lambda n, sh, dt=F32: c.enter_context(nc.sbuf_tensor(n, sh, dt))
        ident, ident16 = identities(nc, s, c)
        logits = sb("logits", [P, TILES, E])
        tops = sb("tops", [P, 2, TILES])
        slots = sb("slots", [P, 2, TILES], U32)
        tile_expert = sb("tile_expert", [P, s["SORTED_TILES"]], I32)
        fill_sorted(nc, s, xsort)
        with ExitStack() as a:
            turned = [P, LB, B, H, HD]
            qT = a.enter_context(nc.sbuf_tensor("qT", turned, F32))
            with ExitStack() as a2:
                ctxT = a2.enter_context(nc.sbuf_tensor("ctxT", turned, F32))
                prologue(nc, s, x, ctx_in, ssm_kernel, dvec, kpad, ctxT, qT, ident)
                convolve(nc, s, kpad, ctxT, qT)
            finish_attention(nc, s, x, qT, gate_w, x2_dram, xs_dram, logits, ident)
        route(nc, s, logits, slots, tops, tile_expert, ident)
        scatter_tokens(nc, s, xs_dram, xsort, slots)
        with ExitStack() as a:
            wsb = lambda n, sh: a.enter_context(nc.sbuf_tensor(n, sh, F16))
            weights = (wsb("gu_hi", [P, E + 2, LB, 2 * F]), wsb("gu_lo", [P, E + 2, LB, 2 * F]),
                       wsb("down_hi", [P, E + 2, s["FB"], L]), wsb("down_lo", [P, E + 2, s["FB"], L]))
            scales = a.enter_context(nc.sbuf_tensor("scales", [P, E + 2, 3], F32))
            split_weights(nc, s, w, *weights, scales)
            expert_tiles(nc, s, 2 * TILES, lambda pair, u: xs_dram[bass.ds(pair * P, P), :],
                         lambda eng, pair, u: E + u, weights, scales, ident16, x2_dram=x2_dram, tag="s_")
            expert_tiles(nc, s, s["SORTED_TILES"], lambda pair, u: xsort[bass.ds((2 * pair + u) * P, P), :],
                         lambda eng, pair, u: eng.value_load(tile_expert[0:1, bass.ds(2 * pair + u, 1)], min_val=0, max_val=E - 1),
                         weights, scales, ident16, y_dram=y_dram, tag="e_")
        combine(nc, s, x2_dram, y_dram, slots, tops, out)


_INS = ["x", "ctx_2048", "L0_xattn_ssm_kernel", "L0_xattn_D", "L0_ffn_gate_w", "L0_ffn_w_gate", "L0_ffn_w_up",
        "L0_ffn_w_down", "L0_ffn_sw_gate", "L0_ffn_sw_up", "L0_ffn_sw_down"]


def kernel(**inputs):
    import numpy as _np
    import concourse.bacc as _bacc
    from concourse import mybir as _mybir
    from concourse.bass_utils import run_bass_kernel_spmd as _run

    nc = _bacc.Bacc("TRN2", target_bir_lowering=False, num_devices=1)
    arrays, args = {}, []
    for name in _INS:
        a = _np.ascontiguousarray(inputs[name])
        arrays[f"in_{name}"] = a
        args.append(nc.dram_tensor(f"in_{name}", a.shape, _mybir.dt.from_np(a.dtype), kind="ExternalInput").ap())
    shape = arrays["in_x"].shape
    args.append(nc.dram_tensor("out_0", shape, _mybir.dt.float32, kind="ExternalOutput").ap())
    build(nc, *args)
    r = _run(nc, [arrays], core_ids=[0])
    return r.results[0]["out_0"]
```

```python
from contextlib import ExitStack

import concourse.bass as bass
from concourse import mybir

F32 = mybir.dt.float32
F32R = mybir.dt.float32r
F16 = mybir.dt.float16
I32 = mybir.dt.int32
U32 = mybir.dt.uint32
ALU = mybir.AluOpType
ACT = mybir.ActivationFunctionType
AX = mybir.AxisListType

P = 128
EPS = 1e-5


def shapes_of(x, ssm_kernel, gate_w, w_gate):
    s = {}
    s["B"], s["CH"], s["L"] = x.shape
    s["H"] = ssm_kernel.shape[0]
    s["HD"] = s["CH"] // s["H"]
    s["E"], _, s["F"] = w_gate.shape
    s["LB"] = s["L"] // P
    s["HALVES"] = s["CH"] // P
    s["HEADS_PER_TILE"] = P // s["HD"]
    s["TOKENS"] = s["B"] * s["CH"]
    s["TILES"] = s["TOKENS"] // P
    return s


def identities(nc, s, ctx):
    ident = ctx.enter_context(nc.sbuf_tensor("ident", [P, P], F32))
    ident16 = ctx.enter_context(nc.sbuf_tensor("ident16", [P, P], F16))
    zeroed = ctx.enter_context(nc.semaphore("ident_zeroed"))
    drawn = ctx.enter_context(nc.semaphore("ident_drawn"))
    with nc.Block() as block:

        @block.gpsimd
        def _(pool):
            pool.memset(ident[:, :], 0.0).then_inc(zeroed, 1)
            pool.wait_ge(zeroed, 1)
            pool.affine_select(out=ident[:, :], in_=ident[:, :], compare_op=ALU.not_equal, fill=1.0,
                               base=0, pattern=[[-1, P]], channel_multiplier=1).then_inc(drawn, 1)

        @block.vector
        def _(dve):
            dve.wait_ge(drawn, 1)
            dve.tensor_copy(ident16[:, :], ident[:, :]).then_inc(zeroed, 1)
    s["passed"] = ctx.enter_context(nc.semaphore("waits_passed"))
    return ident, ident16


def pass_waits(eng, s):
    eng.sem_inc(s["passed"], 1)


def run_skewed(eng, tiles, stages, unroll=2, side=None, peeled=0):
    deepest = max(lag for lag, _ in stages)
    first = max(peeled, -(-deepest // unroll))
    for step in range(first * unroll):
        if side:
            side(step // unroll, step % unroll)
        for lag, stage in stages:
            if step >= lag:
                stage((step - lag) // 2, (step - lag) % 2)
    with eng.Fori(first, tiles // unroll) as turn:
        for k in range(unroll):
            if side:
                side(turn, k)
            for lag, stage in stages:
                stage(turn * (unroll // 2) + (k - lag) // 2, (k - lag) % 2)
    for step in range(tiles, tiles + deepest):
        for lag, stage in stages:
            if step - lag < tiles:
                stage((step - lag) // 2, (step - lag) % 2)


X_SCALE = 1024.0
PEAK = 16384.0
TINY = 1e-30


class SplitPieces:

    def __init__(self, nc, ctx, s, sources, parts, scales, piece_at, tag):
        self.s, self.sources, self.parts, self.scales = s, sources, parts, scales
        self.piece_at = piece_at
        self.F, self.L, self.LB, self.FB = s["F"], s["L"], s["LB"], s["FB"]
        sb = lambda n, sh: ctx.enter_context(nc.sbuf_tensor(tag + n, sh, F32))
        sem = lambda n: ctx.enter_context(nc.semaphore(tag + n))
        self.raw = sb("raw", [P, max(self.LB * self.F, self.FB * self.L)])
        self.peaks, self.peak, self.inv, self.scale = sb("peaks", [P, 2]), sb("peak", [P, 2]), sb("inv", [P, 1]), sb("scale", [P, 1])
        self.loaded, self.peaks_done, self.peak_done, self.chain = sem("loaded"), sem("peaks_done"), sem("peak_done"), sem("chain")
        self.scale_done, self.hi_done, self.lo_done = sem("scale_done"), sem("hi_done"), sem("lo_done")

    def views(self, kind, e):
        F, L, LB, FB = self.F, self.L, self.LB, self.FB
        last = F - (FB - 1) * P
        gu_hi, gu_lo, down_hi, down_lo = self.parts
        if kind < 2:
            at = slice(kind * F, (kind + 1) * F)
            raw = self.raw[:, 0:LB * F].rearrange("p (c f) -> p c f", f=F)
            return [(raw,) + tuple(a[:, bass.ds(e, 1), :, at].rearrange("p a c f -> p (a c) f") for a in (gu_hi, gu_lo))]
        raw = self.raw[:, 0:FB * L].rearrange("p (c l) -> p c l", l=L)
        return [(raw[:, 0:FB - 1, :],) + tuple(a[:, bass.ds(e, 1), 0:FB - 1, :].rearrange("p a c l -> p (a c) l")
                                               for a in (down_hi, down_lo)),
                (raw[0:last, FB - 1:FB, :],) + tuple(a[0:last, bass.ds(e, 1), FB - 1:FB, :].rearrange("p a c l -> p (a c) l")
                                                     for a in (down_hi, down_lo))]

    def pieces(self, what, turn, k):
        found = self.piece_at(what, turn, k)
        return [] if found is None else [(found[0], found[1], 3 * found[0] + found[1])]

    def load(self, eng, turn, k):
        for e, kind, n in self.pieces("load", turn, k):
            eng.wait_ge(self.lo_done, n + 1)
            pass_waits(eng, self.s)
            for (raw, _, _), src in zip(self.views(kind, e), self.sources(kind, e)):
                eng.dma_start(raw, src).then_inc(self.loaded, 16)

    def reduce(self, pool, turn, k):
        for e, kind, n in self.pieces("reduce", turn, k):
            pool.wait_ge(self.peaks_done, n + 1)
            pass_waits(pool, self.s)
            pool.partition_all_reduce(self.peak[:, :], self.peaks[:, :], P, bass.bass_isa.ReduceOp.max)\
                .then_inc(self.peak_done, 1)

    def high(self, act, turn, k):
        for e, kind, n in self.pieces("high", turn, k):
            act.wait_ge(self.scale_done, n + 1)
            for raw, hi, _ in self.views(kind, e):
                last = act.activation(hi, raw, ACT.Copy, scale=self.scale[0:raw.shape[0], :])
            last.then_inc(self.hi_done, 1)

    def peaks_of(self, dve, turn, k):
        if isinstance(turn, int) and turn == 0 and k == 0:
            dve.sem_inc(self.lo_done, 1)
        for e, kind, n in self.pieces("peaks", turn, k):
            dve.wait_ge(self.loaded, 64 * e + (16, 32, 64)[kind])
            if kind < 2:
                dve.memset(self.peaks[:, 1:2], 0.0)
            for m, (raw, _, _) in enumerate(self.views(kind, e)):
                last = dve.tensor_reduce(self.peaks[0:raw.shape[0], m:m + 1], raw, AX.XY, ALU.max, apply_absolute_value=True)
            last.then_inc(self.peaks_done, 1)

    def scale_of(self, dve, turn, k):
        for e, kind, n in self.pieces("scale", turn, k):
            dve.wait_ge(self.peak_done, n + 1)
            dve.tensor_tensor(self.peak[:, 0:1], self.peak[:, 0:1], self.peak[:, 1:2], ALU.max).then_inc(self.chain, 1)
            dve.wait_ge(self.chain, 2 * n + 1)
            dve.tensor_scalar(self.inv[:, :], self.peak[:, 0:1], TINY, 1.0 / PEAK, ALU.max, ALU.mult).then_inc(self.chain, 1)
            dve.wait_ge(self.chain, 2 * n + 2)
            dve.tensor_scalar(self.scales[:, bass.ds(e, 1), kind:kind + 1].rearrange("p a k -> p (a k)"), self.inv[:, :],
                              1.0 / X_SCALE if kind < 2 else 1.0, None, ALU.mult)
            dve.reciprocal(self.scale[:, :], self.inv[:, :]).then_inc(self.scale_done, 1)

    def low_of(self, dve, turn, k):
        for e, kind, n in self.pieces("low", turn, k):
            dve.wait_ge(self.hi_done, n + 1)
            for raw, hi, lo in self.views(kind, e):
                last = dve.scalar_tensor_tensor(lo, raw, self.scale[0:raw.shape[0], :], hi, ALU.mult, ALU.subtract)
            last.then_inc(self.lo_done, 1)

    def low(self, dve, turn, k):
        self.peaks_of(dve, turn, k)
        self.scale_of(dve, turn, k)
        self.low_of(dve, turn, k)


def pad_kernels(nc, s, ssm_kernel, dvec, kpad):
    L, H = s["L"], s["H"]
    with ExitStack() as c:
        kp = c.enter_context(nc.sbuf_tensor("kp", [H, P + L], F32))
        dcol = c.enter_context(nc.sbuf_tensor("dcol", [H, 1], F32))
        loaded, zeroed, added, stored = (c.enter_context(nc.semaphore(f"kp_{n}")) for n in ("loaded", "zeroed", "added", "stored"))
        block = c.enter_context(nc.Block())

        @block.sync
        def _(sp):
            sp.dma_start(kp[:, P:P + L], ssm_kernel).then_inc(loaded, 16)
            sp.dma_start(dcol[:, :], dvec.rearrange("(h a) -> h a", a=1)).then_inc(loaded, 16)
            sp.wait_ge(added, 1)
            sp.wait_ge(zeroed, 1)
            sp.dma_start(kpad[:, :], kp[:, :]).then_inc(stored, 16)
            sp.wait_ge(stored, 16)

        @block.vector
        def _(dve):
            dve.memset(kp[:, 0:P], 0.0).then_inc(zeroed, 1)
            dve.wait_ge(loaded, 32)
            dve.tensor_tensor(kp[:, P:P + 1], kp[:, P:P + 1], dcol[:, :], ALU.add).then_inc(added, 1)


def attention(nc, s, x, ctx_in, gate_w, kpad, x2_dram, xs_dram, xsort, logits, ident, shared_w):
    B, L, LB, H, HD, E, NT = (s[k] for k in ("B", "L", "LB", "H", "HD", "E", "SORTED_TILES"))
    NP = HD * (HD + 1) // 2
    FULL = HD // 2
    EXT = HD + FULL
    HB = B // 2
    ROWS = LB * B
    no = lambda pair, u: 2 * pair + u + 1
    with ExitStack() as c:
        sb = lambda n, sh, dt=F32: c.enter_context(nc.sbuf_tensor("a_" + n, sh, dt))
        psum = lambda n, sh: c.enter_context(nc.psum_tensor("a_" + n, sh, F32))
        sem = lambda n: c.enter_context(nc.semaphore("a_" + n))
        sems = lambda n: [sem(f"{n}{u}") for u in range(2)]
        gate_sb = sb("gate", [P, LB, E])
        zero = sb("zero", [P, 2 * L], F16)
        x_in, x_again, c_in, c_rev, qn = (sb(n, [P, 2, L]) for n in ("x_in", "x_again", "c_in", "c_rev", "qn"))
        toep = sb("toep", [P, 2, L])
        toep_hi, toep_lo = sb("toep_hi", [P, 2, L], F32R), sb("toep_lo", [P, 2, L], F32R)
        kext, qext = sb("kext", [P, 2, ROWS, EXT]), sb("qext", [P, 2, ROWS, EXT])
        kv = sb("kv", [P, ROWS, NP])
        kv_hi, kv_lo = sb("kv_hi", [P, 2, ROWS, NP], F32R), sb("kv_lo", [P, 2, ROWS, NP], F32R)
        prods = sb("prods", [P, LB, B, HD, HD])
        halves = sb("halves", [P, 2, LB, FULL, B * HD])
        x2, xn = sb("x2", [P, 2, L]), sb("xn", [P, 2, L])
        xs = sb("xs", [P, 2, 2, L], F16)
        xnT = sb("xnT", [P, 2, LB, P])
        stats, moments = sb("stats", [P, 2, 2, 6]), sb("moments", [P, 2, 2, 2])
        var_eps, rstd = sb("var_eps", [P, 2, 2, 1]), sb("rstd", [P, 2, 2, 1])
        power = sb("power", [P, 1])
        ps_y = [psum(f"ps_y{v}", [P, 2, 512]) for v in range(2)]
        ps_in = psum("ps_in", [P, LB * P])
        ps_sum = psum("ps_sum", [P, LB * P])
        ps_t = psum("ps_t", [P, LB * P])
        ps_l = psum("ps_l", [P, 512])
        x_loaded, c_loaded, again_loaded, toep_loaded = (sems(n) for n in ("x_loaded", "c_loaded", "again_loaded", "toep_loaded"))
        x2_stored, xs_stored = sems("x2_stored"), sems("xs_stored")
        gate_loaded, filled, zeroed = sem("gate_loaded"), sem("filled"), sem("zeroed")
        q_stats, q_moments, q_eps, q_rstd, q_done = (sem("q_" + n) for n in ("stats", "moments", "eps", "rstd", "done"))
        n_stats, n_moments, n_eps, n_rstd = (sem("n_" + n) for n in ("stats", "moments", "eps", "rstd"))
        c_rev_done, c_turned, q_turned, kext_done, qext_done = (sem(n) for n in ("c_rev", "c_turned", "q_turned", "kext", "qext"))
        toep_hi_done, toep_lo_done, kv_done, kv_hi_done, kv_lo_done = (sem(n) for n in ("toep_hi", "toep_lo", "kv", "kv_hi", "kv_lo"))
        y_done, prods_done, halves_done, summed = (sem(n) for n in ("y", "prods", "halves", "summed"))
        x2_done, xn_done, hi_done, lo_done, xn_turned, xnT_done = (sem(n) for n in ("x2", "xn", "hi", "lo", "xn_turned", "xnT"))
        logits_done, logits_kept = sem("logits"), sem("logits_kept")
        block = c.enter_context(nc.Block())
        split = SplitPieces(nc, c, s, *shared_w, lambda what, turn, k: divmod(2 * turn + k, 3)
                            if isinstance(turn, int) and turn < 3 else None, "a_w_")

        def rows_of(a, pair, u):
            h = 2 * pair + u
            return a[:, bass.ds(HD * h, HD), :]

        @block.sync
        def _(sp):
            sp.dma_start(gate_sb[:, :, :], gate_w.rearrange("(a p) e -> p a e", p=P)).then_inc(gate_loaded, 16)

            def load_c(pair, u):
                sp.wait_ge(c_rev_done, no(pair, u))
                sp.dma_start(c_in[:, u, :], rows_of(ctx_in, pair, u)).then_inc(c_loaded[u], 16)
                sp.wait_ge(toep_lo_done, no(pair, u))
                src = bass.AP(kpad, (2 * pair + u) * (P + L) + 1, [[1, P], [1, L]])
                sp.dma_start(toep[:, u, :], src).then_inc(toep_loaded[u], 16)
                sp.wait_ge(q_done, no(pair, u))
                sp.dma_start(x_in[:, u, :], rows_of(x, pair, u)).then_inc(x_loaded[u], 16)

            def fill(pair, u):
                for k in range(2):
                    sp.dma_start(xsort[bass.ds((2 * (2 * pair + u) + k) * P, P), :], zero[:, :]).then_inc(filled, 16)

            def load_again(pair, u):
                sp.wait_ge(x2_done, no(pair, u))
                sp.dma_start(x_again[:, u, :], rows_of(x, pair, u)).then_inc(again_loaded[u], 16)

            def store_x2(pair, u):
                sp.wait_ge(x2_done, no(pair, u) + 2)
                pass_waits(sp, s)
                sp.dma_start(x2_dram[bass.ds((2 * pair + u) * P, P), :], x2[:, u, :]).then_inc(x2_stored[u], 16)

            def store_xs(pair, u):
                sp.wait_ge(lo_done, no(pair, u) + 2)
                pass_waits(sp, s)
                sp.dma_start(xs_dram[bass.ds((2 * pair + u) * P, P), :], xs[:, u, :, :].rearrange("p a l -> p (a l)"))\
                  .then_inc(xs_stored[u], 16)

            sp.wait_ge(zeroed, 2)
            run_skewed(sp, H, [(0, load_c), (0, fill), (2, load_again), (5, store_x2), (6, store_xs)],
                       side=lambda turn, k: split.load(sp, turn, k))
            for t in range(2 * H, NT):
                sp.dma_start(xsort[t * P:(t + 1) * P, :], zero[:, :]).then_inc(filled, 16)
            sp.wait_ge(filled, 16 * NT)
            for u in range(2):
                sp.wait_ge(x2_stored[u], 16 * (H // 2 + 1))
                sp.wait_ge(xs_stored[u], 16 * (H // 2 + 1))

        @block.gpsimd
        def _(pool):
            pool.memset(zero[:, :], 0.0).then_inc(zeroed, 1)
            pool.memset(power[:, :], -0.5).then_inc(zeroed, 1)
            for u in range(2):
                pool.sem_inc(x2_stored[u], 16)
                pool.sem_inc(xs_stored[u], 16)
            pool.sem_inc(toep_lo_done, 2)
            pool.sem_inc(kv_lo_done, 1)
            pool.sem_inc(halves_done, LB)
            pool.wait_ge(zeroed, 2)

            def rstd_of(which, moments_done, eps_done, rstd_done, done_before):
                def stage(pair, u):
                    n = no(pair, u)
                    pool.wait_ge(moments_done, n)
                    pass_waits(pool, s)
                    pool.tensor_scalar(var_eps[:, which, u, :], moments[:, which, u, 1:2], EPS, None, ALU.add)\
                        .then_inc(eps_done, 1)
                    pool.wait_ge(eps_done, n)
                    pool.tensor_tensor(rstd[:, which, u, :], var_eps[:, which, u, :], power[:, :], ALU.pow)\
                        .then_inc(rstd_done, 1)
                return stage

            def low(pair, u):
                n = no(pair, u)
                pool.wait_ge(toep_hi_done, n)
                pool.wait_ge(y_done, LB * n)
                pool.tensor_tensor(toep_lo[:, u, :], toep[:, u, :], toep_hi[:, u, :].bitcast(F32), ALU.subtract)\
                    .then_inc(toep_lo_done, 1)
                pool.wait_ge(kv_hi_done, n)
                pool.tensor_tensor(kv_lo[:, u, :, :], kv[:, :, :], kv_hi[:, u, :, :].bitcast(F32), ALU.subtract)\
                    .then_inc(kv_lo_done, 1)

            def add_halves(pair, u):
                h = 2 * pair + u
                pool.wait_ge(summed, no(pair, u))
                for lb in range(LB):
                    pool.wait_ge(prods_done, LB * h + lb + 1 + LB + 2)
                    pr = prods[:, lb, :, :, :].rearrange("p b s j -> p s b j")
                    pool.tensor_tensor(halves[:, u, lb, :, :].rearrange("p s (b j) -> p s b j", j=HD), pr[:, 0:FULL],
                                       pr[:, FULL:HD], ALU.add).then_inc(halves_done, 1)

            run_skewed(pool, H, [(4, rstd_of(1, n_moments, n_eps, n_rstd, None)),
                                 (1, rstd_of(0, q_moments, q_eps, q_rstd, None)), (1, low), (2, add_halves)],
                       side=lambda turn, k: split.reduce(pool, turn, k), peeled=3)

        @block.tensor
        def _(pe):
            pe.sem_inc(c_turned, 2)
            pe.sem_inc(q_turned, 2)
            pe.sem_inc(y_done, 2 * LB)
            pe.sem_inc(summed, 2)
            pe.sem_inc(xn_turned, 2)
            pe.sem_inc(logits_done, 2)
            pe.wait_ge(gate_loaded, 16)

            def turn(src, u):
                for lb in range(LB):
                    mm = pe.transpose(ps_in[:, lb * P:(lb + 1) * P], src(lb), ident[:, :])
                return mm

            def turn_c(pair, u):
                n = no(pair, u)
                pe.wait_ge(c_rev_done, n + 2)
                pe.wait_ge(qext_done, n)
                turn(lambda lb: c_rev[:, u, (LB - 1 - lb) * P:(LB - lb) * P], u).then_inc(c_turned, 1)

            def turn_q(pair, u):
                n = no(pair, u)
                pe.wait_ge(q_done, n + 2)
                pe.wait_ge(kext_done, n + 2 + 1)
                turn(lambda lb: qn[:, u, lb * P:(lb + 1) * P], u).then_inc(q_turned, 1)

            def turn_last_q(pair, u):
                pe.wait_ge(q_done, no(pair, u) + 2)
                pe.wait_ge(qext_done, no(pair, u) + 1)
                turn(lambda lb: qn[:, u, lb * P:(lb + 1) * P], u).then_inc(q_turned, 1)

            def convolve(lbs):
                def stage(pair, u):
                    h = 2 * pair + u
                    pe.wait_ge(toep_lo_done, h + 1 + 2)
                    pe.wait_ge(kv_lo_done, h + 1 + 1)
                    for lb in lbs:
                        pe.wait_ge(prods_done, LB * h + lb + 1 + LB)
                        for half in range(2):
                            out = ps_y[lb % 2][:, half, 0:HB * NP]
                            for ib in range(lb + 1):
                                t = slice((lb - ib) * P, (lb - ib + 1) * P)
                                r = slice(ib * B + half * HB, ib * B + (half + 1) * HB)
                                for k, (w, m) in enumerate(((toep_hi, kv_hi), (toep_hi, kv_lo), (toep_lo, kv_hi))):
                                    mm = pe.matmul(out, w[:, u, t], m[:, u, r, :].rearrange("p b n -> p (b n)"),
                                                   start=(ib == 0 and k == 0), stop=(ib == lb and k == 2))
                        mm.then_inc(y_done, 1)
                return stage

            def sum_terms(pair, u):
                h = 2 * pair + u
                pe.wait_ge(x2_done, h + 2)
                pe.wait_ge(halves_done, LB * (h + 1) + LB)
                for lb in range(LB):
                    for k in range(FULL):
                        mm = pe.matmul(ps_sum[:, lb * P:(lb + 1) * P], halves[:, u, lb, k, :], ident[:, :],
                                       start=(k == 0), stop=(k == FULL - 1))
                mm.then_inc(summed, 1)

            def turn_normed(pair, u):
                n = no(pair, u)
                pe.wait_ge(xn_done, n + 2)
                pe.wait_ge(xnT_done, n + 1)
                for lb in range(LB):
                    mm = pe.transpose(ps_t[:, lb * P:(lb + 1) * P], xn[:, u, lb * P:(lb + 1) * P], ident[:, :])
                mm.then_inc(xn_turned, 1)

            def route_logits(pair, u):
                n = no(pair, u)
                pe.wait_ge(xnT_done, n + 2)
                pe.wait_ge(logits_kept, n + 1)
                for lb in range(LB):
                    mm = pe.matmul(ps_l[:, 0:E], xnT[:, u, lb, :], gate_sb[:, lb, :], start=(lb == 0), stop=(lb == LB - 1))
                mm.then_inc(logits_done, 1)

            def q_stage(pair, u):
                last = isinstance(pair, int) and 2 * pair + u == H - 1
                (turn_last_q if last else turn_q)(pair, u)

            run_skewed(pe, H, [(0, turn_c), (5, turn_normed), (2, convolve((0, 1))), (6, route_logits), (2, convolve((2, 3))),
                               (1, q_stage), (3, sum_terms)])

        @block.scalar
        def _(act):
            act.sem_inc(c_rev_done, 2)
            act.sem_inc(kext_done, 2)
            act.sem_inc(qext_done, 2)
            act.sem_inc(xnT_done, 2)

            def backwards(pair, u):
                act.wait_ge(c_loaded[u], 16 * pair + 16)
                act.wait_ge(c_turned, no(pair, u))
                whole = c_in[:, u, L - 1:L]
                act.activation(c_rev[:, u, :], bass.AP(whole.tensor, whole.offset, [whole.ap[0], [-1, L]]), ACT.Copy)\
                   .then_inc(c_rev_done, 1)

            def high(pair, u):
                n = no(pair, u)
                act.wait_ge(toep_loaded[u], 16 * pair + 16)
                act.wait_ge(y_done, LB * n)
                act.activation(toep_hi[:, u, :], toep[:, u, :], ACT.Copy).then_inc(toep_hi_done, 1)
                act.wait_ge(kv_done, n + 2)
                act.activation(kv_hi[:, u, :, :], kv[:, :, :], ACT.Copy).then_inc(kv_hi_done, 1)

            def extend(dst, src, u, done):
                rows = src[:, :].rearrange("p (r j) -> p r j", j=HD)
                act.activation(dst[:, u, :, 0:HD], rows, ACT.Copy)
                act.activation(dst[:, u, :, HD:EXT], rows[:, :, 0:FULL], ACT.Copy).then_inc(done, 1)

            def extend_k(pair, u):
                act.wait_ge(c_turned, no(pair, u) + 2)
                act.wait_ge(kv_done, no(pair, u))
                extend(kext, ps_in, u, kext_done)

            def extend_q(pair, u):
                act.wait_ge(q_turned, no(pair, u) + 2)
                act.wait_ge(prods_done, LB * (2 * pair + u) + 2)
                extend(qext, ps_in, u, qext_done)

            def high_normed(pair, u):
                act.wait_ge(xn_done, no(pair, u) + 2)
                act.wait_ge(xs_stored[u], 16 * pair + 16)
                act.activation(xs[:, u, 0, :], xn[:, u, :], ACT.Copy, scale=X_SCALE).then_inc(hi_done, 1)

            def keep_turned(pair, u):
                act.wait_ge(xn_turned, no(pair, u) + 2)
                act.wait_ge(logits_done, no(pair, u))
                act.activation(xnT[:, u, :, :].rearrange("p a t -> p (a t)"), ps_t[:, :], ACT.Copy).then_inc(xnT_done, 1)

            run_skewed(act, H, [(0, backwards), (0, extend_k), (1, high), (5, keep_turned), (4, high_normed), (1, extend_q)],
                       side=lambda turn, k: split.high(act, turn, k))

        @block.vector
        def _(dve):
            dve.sem_inc(kv_done, 2)
            dve.sem_inc(q_done, 2)
            dve.sem_inc(prods_done, LB + 2)
            dve.sem_inc(x2_done, 2)
            dve.sem_inc(xn_done, 2)
            dve.sem_inc(lo_done, 2)
            dve.sem_inc(logits_kept, 2)

            def statistics(which, src, u, n, stats_done, moments_done):
                dve.bn_stats(stats[:, which, u, :], src).then_inc(stats_done, 1)
                dve.wait_ge(stats_done, n)
                pass_waits(dve, s)
                dve.bn_aggr(moments[:, which, u, :], stats[:, which, u, :]).then_inc(moments_done, 1)

            def add_x(pair, u):
                n = no(pair, u)
                dve.wait_ge(summed, n + 2)
                dve.wait_ge(again_loaded[u], 16 * pair + 16)
                dve.wait_ge(x2_stored[u], 16 * pair + 16)
                dve.tensor_tensor(x2[:, u, :], ps_sum[:, :], x_again[:, u, :], ALU.add).then_inc(x2_done, 1)
                dve.wait_ge(x2_done, n + 2)
                statistics(1, x2[:, u, :], u, n, n_stats, n_moments)

            def read_x(pair, u):
                dve.wait_ge(x_loaded[u], 16 * pair + 16)
                statistics(0, x_in[:, u, :], u, no(pair, u), q_stats, q_moments)

            def products(pair, u):
                n = no(pair, u)
                dve.wait_ge(kext_done, n + 2)
                dve.wait_ge(kv_lo_done, n)
                ke = kext[:, u, :, :]
                first = bass.AP(ke.tensor, ke.offset, [ke.ap[0], [EXT, ROWS], [0, FULL], [1, HD]])
                second = bass.AP(ke.tensor, ke.offset, [ke.ap[0], [EXT, ROWS], [1, FULL], [1, HD]])
                dve.tensor_tensor(kv[:, :, 0:FULL * HD].rearrange("p r (d j) -> p r d j", d=FULL), first, second, ALU.mult)
                dve.tensor_tensor(kv[:, :, FULL * HD:NP], ke[:, :, 0:FULL], ke[:, :, FULL:HD], ALU.mult)\
                   .then_inc(kv_done, 1)

            def norm_q(pair, u):
                n = no(pair, u)
                dve.wait_ge(q_rstd, n)
                dve.wait_ge(q_turned, n)
                dve.tensor_scalar(qn[:, u, :], x_in[:, u, :], moments[:, 0, u, 0:1], rstd[:, 0, u, :],
                                  ALU.subtract, ALU.mult).then_inc(q_done, 1)

            def norm_x2(pair, u):
                n = no(pair, u)
                dve.wait_ge(n_rstd, n)
                dve.wait_ge(xn_turned, n)
                dve.wait_ge(lo_done, n)
                dve.tensor_scalar(xn[:, u, :], x2[:, u, :], moments[:, 1, u, 0:1], rstd[:, 1, u, :],
                                  ALU.subtract, ALU.mult).then_inc(xn_done, 1)

            def low_normed(pair, u):
                dve.wait_ge(hi_done, no(pair, u))
                dve.scalar_tensor_tensor(xs[:, u, 1, :], xn[:, u, :], X_SCALE, xs[:, u, 0, :], ALU.mult,
                                         ALU.subtract).then_inc(lo_done, 1)

            def keep_logits(pair, u):
                dve.wait_ge(logits_done, no(pair, u) + 2)
                dve.tensor_copy(logits[:, bass.ds(2 * pair + u, 1), :].rearrange("p a e -> p (a e)"), ps_l[:, 0:E])\
                   .then_inc(logits_kept, 1)

            def weigh(lbs):
                def stage(pair, u):
                    h = 2 * pair + u
                    dve.wait_ge(qext_done, h + 1 + 2)
                    for lb in lbs:
                        m = LB * h + lb
                        y = ps_y[lb % 2][:, :, 0:HB * NP]
                        q = qext[:, u, lb * B:(lb + 1) * B, :]
                        pr = prods[:, lb, :, :, :]
                        dve.wait_ge(y_done, m + 1 + 2 * LB)
                        dve.wait_ge(halves_done, m + 1)
                        at = lambda a, off, outer, inner, dims: bass.AP(a.tensor, a.offset + off, [a.ap[0], [outer, 2], [inner, HB]] + dims)
                        yat = lambda off, dims: at(y, off, 512, NP, dims)
                        qat = lambda off, dims: at(q, off, EXT * HB, EXT, dims)
                        pat = lambda off, dims: at(pr, off, HD * HD * HB, HD * HD, dims)
                        dve.tensor_tensor(pat(0, [[HD, FULL], [1, HD]]), yat(0, [[HD, FULL], [1, HD]]),
                                          qat(0, [[1, FULL], [1, HD]]), ALU.mult)
                        dve.tensor_tensor(pat(FULL * HD + 1, [[HD + 1, FULL - 1], [1, HD]]),
                                          yat(HD, [[HD, FULL - 1], [1, HD]]),
                                          qat(0, [[0, FULL - 1], [1, HD]]), ALU.mult)
                        dve.tensor_tensor(pat(FULL * HD, [[HD + 1, FULL]]), yat(FULL * HD, [[1, FULL]]),
                                          qat(FULL, [[1, FULL]]), ALU.mult)
                        dve.tensor_tensor(pat(HD * HD - FULL, [[1, FULL]]), yat(FULL * HD, [[1, FULL]]),
                                          qat(0, [[1, FULL]]), ALU.mult).then_inc(prods_done, 1)
                return stage

            run_skewed(dve, H, [(1, products), (1, read_x), (4, add_x), (7, keep_logits), (2, weigh((0, 1))), (1, norm_q),
                                (4, norm_x2), (5, low_normed), (2, weigh((2, 3)))],
                       side=lambda turn, k: split.low(dve, turn, k))


def route(nc, s, logits, slots, tops, tile_expert, ident):
    TILES, E, NT = s["TILES"], s["E"], s["SORTED_TILES"]
    N = TILES * E
    with ExitStack() as c:
        sb = lambda n, sh, dt=F32: c.enter_context(nc.sbuf_tensor(n, sh, dt))
        sem = lambda n: c.enter_context(nc.semaphore(n))
        top = sb("r_top", [P, TILES])
        shifted = sb("r_shifted", [P, TILES, E])
        scores = sb("r_scores", [P, TILES, E])
        rest = sb("r_rest", [P, TILES, E])
        equal = sb("r_equal", [P, TILES, E])
        first = sb("r_first", [P, TILES])
        chosen = sb("r_chosen", [P, 2, TILES, E])
        mask = sb("r_mask", [P, TILES, E])
        expert_no = sb("r_expert_no", [P, E])
        before = sb("r_before", [P, P])
        ones = sb("r_ones", [P, P])
        goes_on = sb("r_goes_on", [P, E, TILES])
        totals = sb("r_totals", [P, E, TILES])
        sums = sb("r_sums", [P, E, TILES])
        starts = sb("r_starts", [P, TILES])
        full = sb("r_full", [P, E, TILES])
        tiles_of = sb("r_tiles_of", [P, E])
        ends = sb("r_ends", [P, E])
        base = sb("r_base", [P, E])
        row = sb("r_row", [P, TILES, E])
        picked = sb("r_picked", [P, TILES, E])
        slot_f = sb("r_slot_f", [P, 2, TILES])
        tile_no = sb("r_tile_no", [P, NT])
        passed = sb("r_passed", [P, NT, E - 1])
        passed_n = sb("r_passed_n", [P, NT])
        ps = c.enter_context(nc.psum_tensor("r_ps", [P, 2, 512], F32))
        drawn, exp_done, exp_ready, step = sem("r_drawn"), sem("r_exp_done"), sem("r_exp_ready"), sem("r_step")
        mask_ready, counted = sem("r_mask_ready"), sem("r_counted")
        block = c.enter_context(nc.Block())

        @block.gpsimd
        def _(pool):
            kw = dict(allow_small_or_imprecise_dtypes=True)
            pool.iota(expert_no[:, :], [[1, E]], base=0, channel_multiplier=0, **kw).then_inc(drawn, 1)
            pool.iota(starts[:, :], [[P, TILES]], base=0, channel_multiplier=0, **kw).then_inc(drawn, 1)
            pool.iota(tile_no[:, :], [[1, NT]], base=0, channel_multiplier=0, **kw).then_inc(drawn, 1)
            pool.memset(ones[:, :], 1.0).then_inc(drawn, 1)
            pool.memset(goes_on[:, :, :], 1.0).then_inc(drawn, 1)
            pool.wait_ge(drawn, 5)
            pool.affine_select(out=before[:, :], in_=ones[:, :], compare_op=ALU.is_gt, fill=0.0, base=0,
                               pattern=[[1, P]], channel_multiplier=-1).then_inc(drawn, 1)
            pool.memset(goes_on[:, :, 0:1], 0.0).then_inc(drawn, 1)

        @block.scalar
        def _(act):
            act.wait_ge(exp_ready, 1)
            act.activation(scores[:, :, :], shifted[:, :, :], ACT.Exp).then_inc(exp_done, 1)

        @block.tensor
        def _(pe):
            pe.wait_ge(mask_ready, 1)
            m = mask[:, :, :].rearrange("p t e -> p (t e)")
            pe.matmul(ps[:, 0, 0:N], before[:, :], m, start=True, stop=True)
            pe.matmul(ps[:, 1, 0:N], ones[:, :], m, start=True, stop=True).then_inc(counted, 1)

        @block.vector
        def _(dve):
            done = [0]

            def then(ins):
                done[0] += 1
                ins.then_inc(step, 1)
                dve.wait_ge(step, done[0])


            each = lambda a: bass.AP(a.tensor, a.offset, [a.ap[0], [1, TILES], [0, E]])
            all_tiles = lambda a: bass.AP(a.tensor, a.offset, [a.ap[0], [0, TILES], [1, E]])
            then(dve.tensor_reduce(top[:, :], logits[:, :, :], AX.X, ALU.max))
            dve.tensor_tensor(shifted[:, :, :], logits[:, :, :], each(top[:, :]), ALU.subtract).then_inc(exp_ready, 1)
            dve.wait_ge(exp_done, 1)
            then(dve.tensor_reduce(top[:, :], scores[:, :, :], AX.X, ALU.add))
            then(dve.reciprocal(first[:, :], top[:, :]))
            then(dve.tensor_tensor(rest[:, :, :], scores[:, :, :], each(first[:, :]), ALU.mult))
            dve.wait_ge(drawn, 7)
            for k in range(2):
                then(dve.tensor_reduce(tops[:, k, :], rest[:, :, :], AX.X, ALU.max))
                then(dve.tensor_tensor(equal[:, :, :], rest[:, :, :], each(tops[:, k, :]), ALU.is_equal))
                then(dve.tensor_scalar(equal[:, :, :], equal[:, :, :], -float(E), float(E), ALU.mult, ALU.add))
                then(dve.tensor_tensor(equal[:, :, :], equal[:, :, :], all_tiles(expert_no[:, :]), ALU.add))
                then(dve.tensor_reduce(first[:, :], equal[:, :, :], AX.X, ALU.min))
                then(dve.tensor_tensor(chosen[:, k, :, :], all_tiles(expert_no[:, :]), each(first[:, :]), ALU.is_equal))
                if k == 0:
                    then(dve.scalar_tensor_tensor(rest[:, :, :], chosen[:, k, :, :], -4.0, rest[:, :, :], ALU.mult, ALU.add))
            dve.tensor_tensor(mask[:, :, :], chosen[:, 0, :, :], chosen[:, 1, :, :], ALU.add).then_inc(mask_ready, 1)
            dve.wait_ge(counted, 1)
            then(dve.tensor_copy(totals[:, :, :], ps[:, 1, 0:N].rearrange("p (t e) -> p e t", e=E)))
            flat = lambda a: a.rearrange("p e t -> p (e t)")
            then(dve.tensor_tensor_scan(flat(sums[:, :, :]), flat(goes_on[:, :, :]), flat(totals[:, :, :]), 0.0,
                                        ALU.mult, ALU.add))
            count = sums[:, :, TILES - 1:TILES]
            then(dve.tensor_tensor(full[:, :, :], bass.AP(count.tensor, count.offset, [count.ap[0], [TILES, E], [0, TILES]]),
                                   bass.AP(starts, 0, [starts[:, :].ap[0], [0, E], [1, TILES]]), ALU.is_gt))
            then(dve.tensor_reduce(tiles_of[:, :], full[:, :, :], AX.X, ALU.add))
            then(dve.tensor_tensor_scan(ends[:, :], ones[:, 0:E], tiles_of[:, :], 0.0, ALU.mult, ALU.add))
            then(dve.tensor_tensor(base[:, :], ends[:, :], tiles_of[:, :], ALU.subtract))
            then(dve.tensor_tensor(sums[:, :, :], sums[:, :, :], totals[:, :, :], ALU.subtract))
            then(dve.scalar_tensor_tensor(row[:, :, :], all_tiles(base[:, :]), float(P),
                                          sums[:, :, :].rearrange("p e t -> p t e"), ALU.mult, ALU.add))
            then(dve.tensor_tensor(row[:, :, :], row[:, :, :], ps[:, 0, 0:N].rearrange("p (t e) -> p t e", e=E), ALU.add))
            for k in range(2):
                then(dve.tensor_tensor(picked[:, :, :], chosen[:, k, :, :], row[:, :, :], ALU.mult))
                then(dve.tensor_reduce(slot_f[:, k, :], picked[:, :, :], AX.X, ALU.add))
            dve.tensor_copy(slots[:, :, :], slot_f[:, :, :])
            then(dve.tensor_tensor(passed[:, :, :], bass.AP(tile_no, 0, [tile_no[:, :].ap[0], [1, NT], [0, E - 1]]),
                                   bass.AP(ends, 0, [ends[:, :].ap[0], [0, NT], [1, E - 1]]), ALU.is_ge))
            then(dve.tensor_reduce(passed_n[:, :], passed[:, :, :], AX.X, ALU.add))
            then(dve.tensor_copy(tile_expert[:, :], passed_n[:, :]))


def expert_tiles(nc, s, tiles, x_rows, expert_of, weights, scales, ident16, tag, y_dram=None, x2_dram=None,
                 xsort=None, slots=None, routed_w=None):
    LB, F, L, FB = s["LB"], s["F"], s["L"], s["FB"]
    LAST = F - (FB - 1) * P
    gu_hi, gu_lo, down_hi, down_lo = weights
    shared = x2_dram is not None
    with ExitStack() as c:
        sb = lambda n, sh, dt=F32: c.enter_context(nc.sbuf_tensor(tag + n, sh, dt))
        psum = lambda n, sh, dt=F32: c.enter_context(nc.psum_tensor(tag + n, sh, dt))
        sem = lambda n: c.enter_context(nc.semaphore(tag + n))
        xs = sb("xs", [P, 2, 2 * LB, P], F16)
        xT = sb("xT", [P, 2, 2 * LB, P], F16)
        gated = sb("gated", [P, 2, F])
        hid = sb("hid", [P, 2, F])
        hpeak, hinv, hscale, yscale = (sb(n, [P, 2, 1]) for n in ("hpeak", "hinv", "hscale", "yscale"))
        h16 = sb("h16", [P, 2, 2, F], F16)
        hT = sb("hT", [P, 2, 2, FB, P], F16)
        y = sb("y", [P, 2, L])
        ps_gu = [psum(f"ps_gu{u}", [P, 2, 512]) for u in range(2)]
        ps_x = psum("ps_x", [P, 2 * LB, P], F16)
        ps_h = psum("ps_h", [P, 2, FB, P], F16)
        ps_y = psum("ps_y", [P, 2, 512])
        loaded = [sem(f"loaded{u}") for u in range(2)]
        stored = [sem(f"stored{u}") for u in range(2)]
        x_turned, xT_done, gate_done, up_done = sem("x_turned"), sem("xT_done"), sem("gate_done"), sem("up_done")
        gated_done, hid_done, small, h_hi_done, h_lo_done = (sem(n) for n in ("gated_done", "hid_done", "small", "h_hi", "h_lo"))
        yscale_done = sem("yscale_done")
        h_turned, hT_done, down_done, y_done = sem("h_turned"), sem("hT_done"), sem("down_done"), sem("y_done")
        unroll = 2
        if shared:
            x2 = sb("x2", [P, L])
            rows_at = sb("rows_at", [P, 2], U32)
            x2_loaded, sent, rows_done = sem("x2_loaded"), sem("sent"), sem("rows_done")
            unroll = 8
            STEPS = {"load": {0: 0, 3: 1, 6: 2}, "peaks": {0: 0, 3: 1, 6: 2}, "reduce": {0: 0, 3: 1, 6: 2},
                     "scale": {1: 0, 4: 1, 7: 2}, "high": {1: 0, 4: 1, 7: 2}, "low": {2: 0, 5: 1, 7: 2}}
            split = SplitPieces(nc, c, s, *routed_w, lambda what, turn, k: (turn, STEPS[what][k])
                                if k in STEPS[what] and not (isinstance(turn, int) and turn >= s["E"]) else None, tag + "w_")
            side = lambda eng, *works: lambda turn, k: [work(eng, turn, k) for work in works]
        block = c.enter_context(nc.Block())
        no = lambda pair, u: 2 * pair + u + 1

        @block.sync
        def _(sp):
            def load(pair, u):
                sp.wait_ge(x_turned, no(pair, u))
                if shared and u == 0 and not (isinstance(pair, int) and pair == 0):
                    pass_waits(sp, s)
                    sp.wait_ge(sent, 32 * pair)
                sp.dma_start(xs[:, u, :, :].rearrange("p a t -> p (a t)"), x_rows(pair, u)).then_inc(loaded[u], 16)

            def load_x2(pair, u):
                if shared and u == 0:
                    sp.wait_ge(y_done, 2 * pair + 1)
                    sp.dma_start(x2[:, :], x2_dram[bass.ds(pair * P, P), :]).then_inc(x2_loaded, 16)

            def store(pair, u):
                sp.wait_ge(y_done, no(pair, u) + 2)
                pass_waits(sp, s)
                if not shared:
                    sp.dma_start(y_dram[bass.ds((2 * pair + u) * P, P), :], y[:, u, :]).then_inc(stored[u], 16)
                elif u == 1:
                    sp.dma_start(x2_dram[bass.ds(pair * P, P), :], y[:, 1, :]).then_inc(stored[u], 16)

            for u in range(2):
                sp.sem_inc(stored[u], 16)
            run_skewed(sp, tiles, [(0, load), (1, load_x2), (4, store)], unroll)
            for u in range(2):
                if not shared or u == 1:
                    sp.wait_ge(stored[u], 16 * (tiles // 2) + 16)

        @block.gpsimd
        def _(pool):
            def send(pair, u):
                if u == 1:
                    return
                if not (isinstance(pair, int) and pair == 0):
                    pool.wait_ge(sent, 32 * pair)
                    pass_waits(pool, s)
                pool.tensor_copy(rows_at[:, :], slots[:, :, bass.ds(pair, 1)].rearrange("p k a -> p (k a)"))\
                    .then_inc(rows_done, 1)
                pool.wait_ge(rows_done, pair + 1)
                pool.wait_ge(loaded[0], 16 * pair + 16)
                pass_waits(pool, s)
                for k in range(2):
                    pool.indirect_dma_start(
                        out=xsort[:, :], out_offset=bass.IndirectOffsetOnAxis(ap=rows_at[:, k:k + 1], axis=0),
                        in_=xs[:, 0, :, :].rearrange("p a t -> p (a t)"), in_offset=None).then_inc(sent, 16)

            if shared:
                run_skewed(pool, tiles, [(0, send)], unroll, side(pool, split.load, split.reduce))
                pool.wait_ge(sent, 16 * tiles)

        @block.tensor
        def _(pe):
            experts = {}

            def turn_x(pair, u):
                pe.wait_ge(loaded[u], 16 * pair + 16)
                pe.wait_ge(xT_done, no(pair, u) + 1)
                for n in range(2 * LB):
                    mm = pe.transpose(ps_x[:, n, :], xs[:, u, n, :], ident16[:, :])
                mm.then_inc(x_turned, 1)

            def project(pair, u, k, ready, done):
                e = experts[u]
                out = ps_gu[u][:, k, 0:F]
                for kb in range(LB):
                    for n, (a, b) in enumerate(((0, gu_hi), (0, gu_lo), (1, gu_hi))):
                        mm = pe.matmul(out, xT[:, u, a * LB + kb, :],
                                       b[:, bass.ds(e, 1), kb, k * F:(k + 1) * F].rearrange("p a f -> p (a f)"),
                                       start=(kb == 0 and n == 0), stop=(kb == LB - 1 and n == 2))
                mm.then_inc(done, 1)

            def gate(pair, u):
                experts[u] = expert_of(pe, pair, u)
                pe.wait_ge(xT_done, no(pair, u) + 2)
                pe.wait_ge(hid_done, no(pair, u))
                project(pair, u, 0, None, gate_done)

            def up(pair, u):
                project(pair, u, 1, None, up_done)

            def turn_h(pair, u):
                pe.wait_ge(h_lo_done, no(pair, u))
                pe.wait_ge(hT_done, no(pair, u) + 1)
                for part in range(2):
                    for fb in range(FB):
                        rows = P if fb < FB - 1 else LAST
                        mm = pe.transpose(ps_h[0:rows, part, fb, :], h16[:, u, part, fb * P:fb * P + rows], ident16[:, :])
                mm.then_inc(h_turned, 1)

            def down(pair, u):
                e = down_expert[u]
                pe.wait_ge(hT_done, no(pair, u) + 2)
                pe.wait_ge(y_done, no(pair, u))
                for fb in range(FB):
                    rows = P if fb < FB - 1 else LAST
                    for n, (a, b) in enumerate(((0, down_hi), (0, down_lo), (1, down_hi))):
                        mm = pe.matmul(ps_y[:, u, :], hT[0:rows, u, a, fb, :],
                                       b[0:rows, bass.ds(e, 1), fb, :].rearrange("p a f -> p (a f)"),
                                       start=(fb == 0 and n == 0), stop=(fb == FB - 1 and n == 2))
                mm.then_inc(down_done, 1)

            down_expert = {}

            def pick_down(pair, u):
                down_expert[u] = expert_of(pe, pair, u)

            pe.sem_inc(x_turned, 2)
            run_skewed(pe, tiles, [(0, turn_x), (1, gate), (2, turn_h), (1, up), (2, pick_down), (2, down)], unroll)

        @block.scalar
        def _(act):
            def swish(pair, u):
                e = expert_of(act, pair, u)
                act.wait_ge(gate_done, no(pair, u))
                act.wait_ge(hid_done, no(pair, u))
                act.activation(gated[:, u, :], ps_gu[u][:, 0, 0:F], ACT.Silu,
                               scale=scales[:, bass.ds(e, 1), 0:1].rearrange("p a k -> p (a k)")).then_inc(gated_done, 1)

            def high(pair, u):
                act.wait_ge(small, 3 * no(pair, u))
                act.wait_ge(h_turned, no(pair, u))
                act.activation(h16[:, u, 0, :], hid[:, u, :], ACT.Copy, scale=hscale[:, u, :]).then_inc(h_hi_done, 1)

            def keep_hT(pair, u):
                act.wait_ge(h_turned, no(pair, u) + 2)
                act.wait_ge(down_done, no(pair, u))
                act.activation(hT[:, u, :, 0:FB - 1, :], ps_h[:, :, 0:FB - 1, :], ACT.Copy)
                act.activation(hT[0:LAST, u, :, FB - 1, :], ps_h[0:LAST, :, FB - 1, :], ACT.Copy).then_inc(hT_done, 1)

            def result(pair, u):
                if shared:
                    return
                act.wait_ge(down_done, no(pair, u) + 2)
                act.wait_ge(yscale_done, no(pair, u))
                act.wait_ge(stored[u], 16 * pair + 16)
                act.activation(y[:, u, :], ps_y[:, u, :], ACT.Copy, scale=yscale[:, u, :]).then_inc(y_done, 1)

            act.sem_inc(hT_done, 2)
            if not shared:
                act.sem_inc(y_done, 2)
            run_skewed(act, tiles, [(2, keep_hT), (1, swish), (1, high), (2, result)], unroll,
                       side(act, split.high) if shared else None)

        @block.vector
        def _(dve):
            def keep_xT(pair, u):
                dve.wait_ge(x_turned, no(pair, u) + 2)
                dve.wait_ge(up_done, no(pair, u))
                dve.tensor_copy(xT[:, u, :, :], ps_x[:, :, :]).then_inc(xT_done, 1)

            def hidden(pair, u):
                e = expert_of(dve, pair, u)
                n = no(pair, u)
                dve.wait_ge(up_done, n + 2)
                dve.wait_ge(gated_done, n)
                dve.scalar_tensor_tensor(hid[:, u, :], ps_gu[u][:, 1, 0:F],
                                         scales[:, bass.ds(e, 1), 1:2].rearrange("p a k -> p (a k)"),
                                         gated[:, u, :], ALU.mult, ALU.mult).then_inc(hid_done, 1)
                dve.wait_ge(hid_done, n + 2)
                dve.tensor_reduce(hpeak[:, u, :], hid[:, u, :], AX.X, ALU.max, apply_absolute_value=True).then_inc(small, 1)
                dve.wait_ge(small, 3 * n - 2)
                dve.tensor_scalar(hinv[:, u, :], hpeak[:, u, :], TINY, 1.0 / PEAK, ALU.max, ALU.mult).then_inc(small, 1)
                dve.wait_ge(small, 3 * n - 1)
                dve.reciprocal(hscale[:, u, :], hinv[:, u, :]).then_inc(small, 1)
                dve.wait_ge(y_done, n)
                dve.tensor_tensor(yscale[:, u, :], hinv[:, u, :],
                                  scales[:, bass.ds(e, 1), 2:3].rearrange("p a k -> p (a k)"), ALU.mult)\
                   .then_inc(yscale_done, 1)
                dve.wait_ge(h_hi_done, n)
                dve.scalar_tensor_tensor(h16[:, u, 1, :], hid[:, u, :], hscale[:, u, :], h16[:, u, 0, :], ALU.mult,
                                         ALU.subtract).then_inc(h_lo_done, 1)

            def result(pair, u):
                if not shared:
                    return
                n = no(pair, u)
                dve.wait_ge(down_done, n + 2)
                dve.wait_ge(yscale_done, n)
                if u == 0:
                    dve.wait_ge(x2_loaded, 16 * pair + 16)
                    dve.wait_ge(y_done, n + 1)
                    src = x2[:, :]
                else:
                    dve.wait_ge(y_done, n + 1)
                    dve.wait_ge(stored[1], 16 * pair + 16)
                    src = y[:, 0, :]
                dve.scalar_tensor_tensor(y[:, u, :], ps_y[:, u, :], yscale[:, u, :], src, ALU.mult, ALU.add)\
                   .then_inc(y_done, 1)

            dve.sem_inc(xT_done, 2)
            dve.sem_inc(up_done, 2)
            dve.sem_inc(hid_done, 2)
            dve.sem_inc(h_turned, 2)
            dve.sem_inc(down_done, 2)
            if shared:
                dve.sem_inc(y_done, 2)
            run_skewed(dve, tiles, [(0, keep_xT), (1, hidden), (2, result)], unroll,
                       side(dve, split.peaks_of, split.scale_of, split.low_of) if shared else None)


def combine(nc, s, r_dram, y_dram, slots, tops, out):
    TILES, L = s["TILES"], s["L"]
    SL = 4
    with ExitStack() as c:
        sb = lambda n, sh, dt=F32: c.enter_context(nc.sbuf_tensor("c_" + n, sh, dt))
        sem = lambda n: c.enter_context(nc.semaphore("c_" + n))
        r = sb("r", [P, SL, L])
        g = sb("g", [P, SL, 2, L])
        acc = sb("acc", [P, SL, L])
        o = sb("o", [P, SL, L])
        r_loaded, g_loaded, stored = ([sem(f"{n}{u}") for u in range(SL)] for n in ("r_loaded", "g_loaded", "stored"))
        first_done, out_done = sem("first_done"), sem("out_done")
        block = c.enter_context(nc.Block())
        rows = lambda a, t: a[t * P:(t + 1) * P, :]
        out_rows = lambda t: out[:, t * s["HD"]:(t + 1) * s["HD"], :]

        @block.sync
        def _(sp):
            for t in range(TILES + 2):
                if t < TILES:
                    if t >= SL:
                        sp.wait_ge(first_done, t - SL + 1)
                    sp.dma_start(r[:, t % SL, :], rows(r_dram, t)).then_inc(r_loaded[t % SL], 16)
                if t >= 2:
                    sp.wait_ge(out_done, t - 1)
                    sp.dma_start(out_rows(t - 2), o[:, (t - 2) % SL, :]).then_inc(stored[(t - 2) % SL], 16)
            for u in range(SL):
                sp.wait_ge(stored[u], 16 * (TILES // SL))

        @block.gpsimd
        def _(pool):
            for t in range(TILES):
                if t >= SL:
                    pool.wait_ge(out_done, t - SL + 1)
                for k in range(2):
                    pool.indirect_dma_start(out=g[:, t % SL, k, :], out_offset=None, in_=y_dram[:, :],
                                            in_offset=bass.IndirectOffsetOnAxis(ap=slots[:, k, t:t + 1], axis=0))\
                        .then_inc(g_loaded[t % SL], 16)

        @block.vector
        def _(dve):
            for t in range(TILES):
                u = t % SL
                dve.wait_ge(r_loaded[u], 16 * (t // SL + 1))
                dve.wait_ge(g_loaded[u], 32 * (t // SL + 1))
                dve.scalar_tensor_tensor(acc[:, u, :], g[:, u, 0, :], tops[:, 0, t:t + 1], r[:, u, :], ALU.mult, ALU.add)\
                   .then_inc(first_done, 1)
                dve.wait_ge(first_done, t + 1)
                if t >= SL:
                    dve.wait_ge(stored[u], 16 * (t // SL))
                dve.scalar_tensor_tensor(o[:, u, :], g[:, u, 1, :], tops[:, 1, t:t + 1], acc[:, u, :], ALU.mult, ALU.add)\
                   .then_inc(out_done, 1)


def build(nc, x, ctx_in, ssm_kernel, dvec, gate_w, w_gate, w_up, w_down, sw_gate, sw_up, sw_down, out):
    s = shapes_of(x, ssm_kernel, gate_w, w_gate)
    B, L, LB, H, HD, E, F, TILES = (s[k] for k in ("B", "L", "LB", "H", "HD", "E", "F", "TILES"))
    s["FB"] = -(-F // P)
    s["SORTED_TILES"] = 2 * TILES + E
    w = {"gate": w_gate, "up": w_up, "down": w_down, "s_gate": sw_gate, "s_up": sw_up, "s_down": sw_down}
    kpad = nc.dram_tensor("kpad", [H, P + L], F32)
    x2_dram = nc.dram_tensor("x2_rows", [s["TOKENS"], L], F32)
    xs_dram = nc.dram_tensor("xs_rows", [s["TOKENS"], 2 * L], F16)
    xsort = nc.dram_tensor("x_sorted", [s["SORTED_TILES"] * P, 2 * L], F16)
    y_dram = nc.dram_tensor("y_sorted", [s["SORTED_TILES"] * P, L], F32)
    whole = (s["FB"] - 1) * P

    def in_parts(kind, w):
        if kind < 2:
            return [w.rearrange("(c p) f -> p c f", p=P)]
        return [w[0:whole, :].rearrange("(c p) l -> p c l", p=P), w[whole:F, :].rearrange("(c p) l -> p c l", c=1)]

    def shared_sources(kind, e):
        half = slice(e * F, (e + 1) * F)
        return in_parts(kind, sw_down[half, :] if kind == 2 else (sw_gate, sw_up)[kind][:, half])

    def routed_sources(kind, e):
        return in_parts(kind, (w_gate, w_up, w_down)[kind][bass.ds(e, 1), :, :].rearrange("a k n -> (a k) n"))

    with ExitStack() as c:
        sb = lambda n, sh, dt=F32: c.enter_context(nc.sbuf_tensor(n, sh, dt))
        ident, ident16 = identities(nc, s, c)
        logits = sb("logits", [P, TILES, E])
        tops = sb("tops", [P, 2, TILES])
        slots = sb("slots", [P, 2, TILES], U32)
        tile_expert = sb("tile_expert", [P, s["SORTED_TILES"]], I32)
        scales = sb("scales", [P, E, 3])
        shared_scales = sb("shared_scales", [P, 2, 3])

        def split_buffers(ctx, tag, n):
            return tuple(ctx.enter_context(nc.sbuf_tensor(tag + m, sh, F16)) for m, sh in (
                ("gu_hi", [P, n, LB, 2 * F]), ("gu_lo", [P, n, LB, 2 * F]),
                ("down_hi", [P, n, s["FB"], L]), ("down_lo", [P, n, s["FB"], L])))

        pad_kernels(nc, s, ssm_kernel, dvec, kpad)
        with ExitStack() as a:
            shared_parts = split_buffers(a, "shared_", 2)
            attention(nc, s, x, ctx_in, gate_w, kpad, x2_dram, xs_dram, xsort, logits, ident,
                      (shared_sources, shared_parts, shared_scales))
            route(nc, s, logits, slots, tops, tile_expert, ident)
            parts = split_buffers(a, "", E)
            expert_tiles(nc, s, 2 * TILES, lambda pair, u: xs_dram[bass.ds(pair * P, P), :], lambda eng, pair, u: u,
                         shared_parts, shared_scales, ident16, "s_", x2_dram=x2_dram, xsort=xsort, slots=slots,
                         routed_w=(routed_sources, parts, scales))
            expert_tiles(nc, s, s["SORTED_TILES"], lambda pair, u: xsort[bass.ds((2 * pair + u) * P, P), :],
                         lambda eng, pair, u: eng.value_load(tile_expert[0:1, bass.ds(2 * pair + u, 1)], min_val=0, max_val=E - 1),
                         parts, scales, ident16, "e_", y_dram=y_dram)
        combine(nc, s, x2_dram, y_dram, slots, tops, out)


_INS = ["x", "ctx_2048", "L0_xattn_ssm_kernel", "L0_xattn_D", "L0_ffn_gate_w", "L0_ffn_w_gate", "L0_ffn_w_up",
        "L0_ffn_w_down", "L0_ffn_sw_gate", "L0_ffn_sw_up", "L0_ffn_sw_down"]


def kernel(**inputs):
    import numpy as _np
    import concourse.bacc as _bacc
    from concourse import mybir as _mybir
    from concourse.bass_utils import run_bass_kernel_spmd as _run

    nc = _bacc.Bacc("TRN2", target_bir_lowering=False, num_devices=1)
    arrays, args = {}, []
    for name in _INS:
        a = _np.ascontiguousarray(inputs[name])
        arrays[f"in_{name}"] = a
        args.append(nc.dram_tensor(f"in_{name}", a.shape, _mybir.dt.from_np(a.dtype), kind="ExternalInput").ap())
    shape = arrays["in_x"].shape
    args.append(nc.dram_tensor("out_0", shape, _mybir.dt.float32, kind="ExternalOutput").ap())
    build(nc, *args)
    r = _run(nc, [arrays], core_ids=[0])
    return r.results[0]["out_0"]
```

```python
from contextlib import ExitStack

import concourse.bass as bass
from concourse import mybir

F32 = mybir.dt.float32
F32R = mybir.dt.float32r
F16 = mybir.dt.float16
I32 = mybir.dt.int32
U32 = mybir.dt.uint32
ALU = mybir.AluOpType
ACT = mybir.ActivationFunctionType
AX = mybir.AxisListType

P = 128
EPS = 1e-5


def shapes_of(x, ssm_kernel, gate_w, w_gate):
    s = {}
    s["B"], s["CH"], s["L"] = x.shape
    s["H"] = ssm_kernel.shape[0]
    s["HD"] = s["CH"] // s["H"]
    s["E"], _, s["F"] = w_gate.shape
    s["LB"] = s["L"] // P
    s["HALVES"] = s["CH"] // P
    s["HEADS_PER_TILE"] = P // s["HD"]
    s["TOKENS"] = s["B"] * s["CH"]
    s["TILES"] = s["TOKENS"] // P
    return s


def identities(nc, s, ctx):
    ident = ctx.enter_context(nc.sbuf_tensor("ident", [P, P], F32))
    ident16 = ctx.enter_context(nc.sbuf_tensor("ident16", [P, P], F16))
    zeroed = ctx.enter_context(nc.semaphore("ident_zeroed"))
    drawn = ctx.enter_context(nc.semaphore("ident_drawn"))
    with nc.Block() as block:

        @block.gpsimd
        def _(pool):
            pool.memset(ident[:, :], 0.0).then_inc(zeroed, 1)
            pool.wait_ge(zeroed, 1)
            pool.affine_select(out=ident[:, :], in_=ident[:, :], compare_op=ALU.not_equal, fill=1.0,
                               base=0, pattern=[[-1, P]], channel_multiplier=1).then_inc(drawn, 1)

        @block.vector
        def _(dve):
            dve.wait_ge(drawn, 1)
            dve.tensor_copy(ident16[:, :], ident[:, :]).then_inc(zeroed, 1)
    s["passed"] = ctx.enter_context(nc.semaphore("waits_passed"))
    return ident, ident16


def pass_waits(eng, s):
    eng.sem_inc(s["passed"], 1)


def run_skewed(eng, tiles, stages, unroll=2, peeled=0):
    deepest = max(lag or 0 for lag, _ in stages)
    first = max(peeled, -(-deepest // unroll))

    def outside(step):
        for lag, stage in stages:
            if lag is None or lag <= step < tiles + lag:
                stage((step - (lag or 0)) // unroll, (step - (lag or 0)) % unroll)

    for step in range(first * unroll):
        outside(step)
    if first < tiles // unroll:
        with eng.Fori(first, tiles // unroll) as turn:
            for k in range(unroll):
                for lag, stage in stages:
                    stage(turn + (k - (lag or 0)) // unroll, (k - (lag or 0)) % unroll)
    for step in range(tiles, tiles + deepest):
        outside(step)


X_SCALE = 1024.0
PEAK = 16384.0
TINY = 1e-30


class SplitPieces:

    def __init__(self, nc, ctx, s, sources, parts, scales, piece_at, tag):
        self.s, self.sources, self.parts, self.scales = s, sources, parts, scales
        self.piece_at = piece_at
        self.F, self.L, self.LB, self.FB = s["F"], s["L"], s["LB"], s["FB"]
        sb = lambda n, sh: ctx.enter_context(nc.sbuf_tensor(tag + n, sh, F32))
        sem = lambda n: ctx.enter_context(nc.semaphore(tag + n))
        self.raw = sb("raw", [P, max(self.LB * self.F, self.FB * self.L)])
        self.peaks, self.peak = sb("peaks", [P, 2]), sb("peak", [P, 2])
        self.inv, self.scale = sb("inv", [P, 1]), sb("scale", [P, 1])
        self.loaded, self.peaks_done, self.peak_done = sem("loaded"), sem("peaks_done"), sem("peak_done")
        self.chain = sem("chain")
        self.scale_done, self.hi_done, self.lo_done = sem("scale_done"), sem("hi_done"), sem("lo_done")

    def views(self, kind, e):
        F, L, LB, FB = self.F, self.L, self.LB, self.FB
        last = F - (FB - 1) * P
        gu_hi, gu_lo, down_hi, down_lo = self.parts
        if kind < 2:
            at = slice(kind * F, (kind + 1) * F)
            raw = self.raw[:, 0:LB * F].rearrange("p (c f) -> p c f", f=F)
            return [(raw,) + tuple(a[:, bass.ds(e, 1), :, at].rearrange("p a c f -> p (a c) f") for a in (gu_hi, gu_lo))]
        raw = self.raw[:, 0:FB * L].rearrange("p (c l) -> p c l", l=L)
        return [(raw[:, 0:FB - 1, :],) + tuple(a[:, bass.ds(e, 1), 0:FB - 1, :].rearrange("p a c l -> p (a c) l")
                                               for a in (down_hi, down_lo)),
                (raw[0:last, FB - 1:FB, :],) + tuple(a[0:last, bass.ds(e, 1), FB - 1:FB, :].rearrange("p a c l -> p (a c) l")
                                                     for a in (down_hi, down_lo))]

    def pieces(self, what, turn, k):
        found = self.piece_at(what, turn, k)
        return [] if found is None else [(found[0], found[1], 3 * found[0] + found[1])]

    def load(self, eng, turn, k):
        for e, kind, n in self.pieces("load", turn, k):
            eng.wait_ge(self.lo_done, n + 1)
            pass_waits(eng, self.s)
            for (raw, _, _), src in zip(self.views(kind, e), self.sources(kind, e)):
                eng.dma_start(raw, src).then_inc(self.loaded, 16)

    def reduce(self, pool, turn, k):
        for e, kind, n in self.pieces("reduce", turn, k):
            pool.wait_ge(self.peaks_done, n + 1)
            pass_waits(pool, self.s)
            pool.partition_all_reduce(self.peak[:, :], self.peaks[:, :], P, bass.bass_isa.ReduceOp.max)\
                .then_inc(self.peak_done, 1)

    def high(self, act, turn, k):
        for e, kind, n in self.pieces("high", turn, k):
            act.wait_ge(self.scale_done, n + 1)
            for raw, hi, _ in self.views(kind, e):
                last = act.activation(hi, raw, ACT.Copy, scale=self.scale[0:raw.shape[0], :])
            last.then_inc(self.hi_done, 1)

    def peaks_of(self, dve, turn, k):
        if isinstance(turn, int) and turn == 0 and k == 0:
            dve.sem_inc(self.lo_done, 1)
        for e, kind, n in self.pieces("peaks", turn, k):
            dve.wait_ge(self.loaded, 64 * e + (16, 32, 64)[kind])
            if kind < 2:
                dve.memset(self.peaks[:, 1:2], 0.0)
            for m, (raw, _, _) in enumerate(self.views(kind, e)):
                last = dve.tensor_reduce(self.peaks[0:raw.shape[0], m:m + 1], raw, AX.XY, ALU.max, apply_absolute_value=True)
            last.then_inc(self.peaks_done, 1)

    def scale_of(self, dve, turn, k):
        for e, kind, n in self.pieces("scale", turn, k):
            dve.wait_ge(self.peak_done, n + 1)
            dve.tensor_tensor(self.peak[:, 0:1], self.peak[:, 0:1], self.peak[:, 1:2], ALU.max).then_inc(self.chain, 1)
            dve.wait_ge(self.chain, 2 * n + 1)
            dve.tensor_scalar(self.inv[:, :], self.peak[:, 0:1], TINY, 1.0 / PEAK, ALU.max, ALU.mult).then_inc(self.chain, 1)
            dve.wait_ge(self.chain, 2 * n + 2)
            dve.tensor_scalar(self.scales[:, bass.ds(e, 1), kind:kind + 1].rearrange("p a k -> p (a k)"), self.inv[:, :],
                              1.0 / X_SCALE if kind < 2 else 1.0, None, ALU.mult)
            dve.reciprocal(self.scale[:, :], self.inv[:, :]).then_inc(self.scale_done, 1)

    def low_of(self, dve, turn, k):
        for e, kind, n in self.pieces("low", turn, k):
            dve.wait_ge(self.hi_done, n + 1)
            for raw, hi, lo in self.views(kind, e):
                last = dve.scalar_tensor_tensor(lo, raw, self.scale[0:raw.shape[0], :], hi, ALU.mult, ALU.subtract)
            last.then_inc(self.lo_done, 1)


def pad_kernels(nc, s, ssm_kernel, dvec, kpad):
    L, H = s["L"], s["H"]
    with ExitStack() as c:
        kp = c.enter_context(nc.sbuf_tensor("kp", [H, P + L], F32))
        parts = c.enter_context(nc.sbuf_tensor("kp_parts", [H, 2, P + L], F32R))
        dcol = c.enter_context(nc.sbuf_tensor("dcol", [H, 1], F32))
        loaded, zeroed, added, high_done, low_done, stored = (
            c.enter_context(nc.semaphore(f"kp_{n}")) for n in ("loaded", "zeroed", "added", "high", "low", "stored"))
        block = c.enter_context(nc.Block())

        @block.sync
        def _(sp):
            sp.dma_start(kp[:, P:P + L], ssm_kernel).then_inc(loaded, 16)
            sp.dma_start(dcol[:, :], dvec.rearrange("(h a) -> h a", a=1)).then_inc(loaded, 16)
            sp.wait_ge(low_done, 1)
            sp.dma_start(kpad[:, :, :].rearrange("a h l -> h a l"), parts[:, :, :].bitcast(F32)).then_inc(stored, 16)
            sp.wait_ge(stored, 16)

        @block.vector
        def _(dve):
            dve.memset(kp[:, 0:P], 0.0).then_inc(zeroed, 1)
            dve.wait_ge(loaded, 32)
            dve.tensor_tensor(kp[:, P:P + 1], kp[:, P:P + 1], dcol[:, :], ALU.add).then_inc(added, 1)

        @block.scalar
        def _(act):
            act.wait_ge(zeroed, 1)
            act.wait_ge(added, 1)
            act.activation(parts[:, 0, :], kp[:, :], ACT.Copy).then_inc(high_done, 1)

        @block.gpsimd
        def _(pool):
            pool.wait_ge(high_done, 1)
            pool.tensor_tensor(parts[:, 1, :], kp[:, :], parts[:, 0, :].bitcast(F32), ALU.subtract).then_inc(low_done, 1)


class Router:

    def __init__(self, nc, c, s, logits, slots, tops, tile_expert, ps_before, ps_whole):
        TILES, E, NT = self.TILES, self.E, self.NT = s["TILES"], s["E"], s["SORTED_TILES"]
        self.logits, self.slots, self.tops, self.tile_expert = logits, slots, tops, tile_expert
        self.ps_before, self.ps_whole = ps_before, ps_whole
        sb = lambda n, sh, dt=F32: c.enter_context(nc.sbuf_tensor("r_" + n, sh, dt))
        sem = lambda n: c.enter_context(nc.semaphore("r_" + n))
        self.top = sb("top", [P, TILES])
        self.shifted = sb("shifted", [P, TILES, E])
        self.scores = sb("scores", [P, TILES, E])
        self.rest = sb("rest", [P, TILES, E])
        self.equal = sb("equal", [P, TILES, E])
        self.first = sb("first", [P, TILES])
        self.chosen = sb("chosen", [P, 2, TILES, E])
        self.mask = sb("mask", [P, TILES, E])
        self.expert_no = sb("expert_no", [P, E])
        self.before = sb("before", [P, P])
        self.ones = sb("ones", [P, P])
        self.goes_on = sb("goes_on", [P, E, TILES])
        self.totals = sb("totals", [P, E, TILES])
        self.sums = sb("sums", [P, E, TILES])
        self.starts = sb("starts", [P, TILES])
        self.full = sb("full", [P, E, TILES])
        self.tiles_of = sb("tiles_of", [P, E])
        self.ends = sb("ends", [P, E])
        self.base = sb("base", [P, E])
        self.row = sb("row", [P, TILES, E])
        self.picked = sb("picked", [P, TILES, E])
        self.slot_f = sb("slot_f", [P, 2, TILES])
        self.tile_no = sb("tile_no", [P, NT])
        self.passed = sb("passed", [P, NT, E - 1])
        self.passed_n = sb("passed_n", [P, NT])
        self.drawn = sem("drawn")
        self.exp_done = sem("exp_done")
        self.exp_ready = sem("exp_ready")
        self.step = sem("step")
        self.mask_ready = sem("mask_ready")
        self.counted = sem("counted")

    def draw(self, pool):
        TILES, E, NT = self.TILES, self.E, self.NT
        kw = dict(allow_small_or_imprecise_dtypes=True)
        pool.iota(self.expert_no[:, :], [[1, E]], base=0, channel_multiplier=0, **kw).then_inc(self.drawn, 1)
        pool.iota(self.starts[:, :], [[P, TILES]], base=0, channel_multiplier=0, **kw).then_inc(self.drawn, 1)
        pool.iota(self.tile_no[:, :], [[1, NT]], base=0, channel_multiplier=0, **kw).then_inc(self.drawn, 1)
        pool.memset(self.ones[:, :], 1.0).then_inc(self.drawn, 1)
        pool.memset(self.goes_on[:, :, :], 1.0).then_inc(self.drawn, 1)
        pool.wait_ge(self.drawn, 5)
        pool.affine_select(out=self.before[:, :], in_=self.ones[:, :], compare_op=ALU.is_gt, fill=0.0, base=0,
                           pattern=[[1, P]], channel_multiplier=-1).then_inc(self.drawn, 1)
        pool.memset(self.goes_on[:, :, 0:1], 0.0).then_inc(self.drawn, 1)

    def exponents(self, act):
        act.wait_ge(self.exp_ready, 1)
        act.activation(self.scores[:, :, :], self.shifted[:, :, :], ACT.Exp).then_inc(self.exp_done, 1)

    def count(self, pe):
        N = self.TILES * self.E
        pe.wait_ge(self.mask_ready, 1)
        m = self.mask[:, :, :].rearrange("p t e -> p (t e)")
        pe.matmul(self.ps_before[:, 0:N], self.before[:, :], m, start=True, stop=True)
        pe.matmul(self.ps_whole[:, 0:N], self.ones[:, :], m, start=True, stop=True).then_inc(self.counted, 1)

    def choose(self, dve):
        TILES, E, NT = self.TILES, self.E, self.NT
        N = TILES * E
        logits, slots, tops, tile_expert = self.logits, self.slots, self.tops, self.tile_expert
        done = [0]

        def then(ins):
            done[0] += 1
            ins.then_inc(self.step, 1)
            dve.wait_ge(self.step, done[0])

        each = lambda a: bass.AP(a.tensor, a.offset, [a.ap[0], [1, TILES], [0, E]])
        all_tiles = lambda a: bass.AP(a.tensor, a.offset, [a.ap[0], [0, TILES], [1, E]])
        then(dve.tensor_reduce(self.top[:, :], logits[:, :, :], AX.X, ALU.max))
        dve.tensor_tensor(self.shifted[:, :, :], logits[:, :, :], each(self.top[:, :]), ALU.subtract).then_inc(self.exp_ready, 1)
        dve.wait_ge(self.exp_done, 1)
        then(dve.tensor_reduce(self.top[:, :], self.scores[:, :, :], AX.X, ALU.add))
        then(dve.reciprocal(self.first[:, :], self.top[:, :]))
        then(dve.tensor_tensor(self.rest[:, :, :], self.scores[:, :, :], each(self.first[:, :]), ALU.mult))
        dve.wait_ge(self.drawn, 7)
        for k in range(2):
            then(dve.tensor_reduce(tops[:, k, :], self.rest[:, :, :], AX.X, ALU.max))
            then(dve.tensor_tensor(self.equal[:, :, :], self.rest[:, :, :], each(tops[:, k, :]), ALU.is_equal))
            then(dve.tensor_scalar(self.equal[:, :, :], self.equal[:, :, :], -float(E), float(E), ALU.mult, ALU.add))
            then(dve.tensor_tensor(self.equal[:, :, :], self.equal[:, :, :], all_tiles(self.expert_no[:, :]), ALU.add))
            then(dve.tensor_reduce(self.first[:, :], self.equal[:, :, :], AX.X, ALU.min))
            then(dve.tensor_tensor(self.chosen[:, k, :, :], all_tiles(self.expert_no[:, :]), each(self.first[:, :]), ALU.is_equal))
            if k == 0:
                then(dve.scalar_tensor_tensor(self.rest[:, :, :], self.chosen[:, k, :, :], -4.0, self.rest[:, :, :], ALU.mult, ALU.add))
        dve.tensor_tensor(self.mask[:, :, :], self.chosen[:, 0, :, :], self.chosen[:, 1, :, :], ALU.add).then_inc(self.mask_ready, 1)
        dve.wait_ge(self.counted, 1)
        then(dve.tensor_copy(self.totals[:, :, :], self.ps_whole[:, 0:N].rearrange("p (t e) -> p e t", e=E)))
        flat = lambda a: a.rearrange("p e t -> p (e t)")
        then(dve.tensor_tensor_scan(flat(self.sums[:, :, :]), flat(self.goes_on[:, :, :]), flat(self.totals[:, :, :]), 0.0,
                                    ALU.mult, ALU.add))
        count = self.sums[:, :, TILES - 1:TILES]
        then(dve.tensor_tensor(self.full[:, :, :], bass.AP(count.tensor, count.offset, [count.ap[0], [TILES, E], [0, TILES]]),
                               bass.AP(self.starts, 0, [self.starts[:, :].ap[0], [0, E], [1, TILES]]), ALU.is_gt))
        then(dve.tensor_reduce(self.tiles_of[:, :], self.full[:, :, :], AX.X, ALU.add))
        then(dve.tensor_tensor_scan(self.ends[:, :], self.ones[:, 0:E], self.tiles_of[:, :], 0.0, ALU.mult, ALU.add))
        then(dve.tensor_tensor(self.base[:, :], self.ends[:, :], self.tiles_of[:, :], ALU.subtract))
        then(dve.tensor_tensor(self.sums[:, :, :], self.sums[:, :, :], self.totals[:, :, :], ALU.subtract))
        then(dve.scalar_tensor_tensor(self.row[:, :, :], all_tiles(self.base[:, :]), float(P),
                                      self.sums[:, :, :].rearrange("p e t -> p t e"), ALU.mult, ALU.add))
        then(dve.tensor_tensor(self.row[:, :, :], self.row[:, :, :], self.ps_before[:, 0:N].rearrange("p (t e) -> p t e", e=E), ALU.add))
        for k in range(2):
            then(dve.tensor_tensor(self.picked[:, :, :], self.chosen[:, k, :, :], self.row[:, :, :], ALU.mult))
            then(dve.tensor_reduce(self.slot_f[:, k, :], self.picked[:, :, :], AX.X, ALU.add))
        dve.tensor_copy(slots[:, :, :], self.slot_f[:, :, :])
        then(dve.tensor_tensor(self.passed[:, :, :], bass.AP(self.tile_no, 0, [self.tile_no[:, :].ap[0], [1, NT], [0, E - 1]]),
                               bass.AP(self.ends, 0, [self.ends[:, :].ap[0], [0, NT], [1, E - 1]]), ALU.is_ge))
        then(dve.tensor_reduce(self.passed_n[:, :], self.passed[:, :, :], AX.X, ALU.add))
        then(dve.tensor_copy(tile_expert[:, :], self.passed_n[:, :]))


def attention(nc, s, x, ctx_in, gate_w, kpad, x2_dram, xn_dram, xT_dram, xsort, logits, slots, tops, tile_expert,
              ident, shared_w):
    B, L, LB, H, HD, E, NT = (s[k] for k in ("B", "L", "LB", "H", "HD", "E", "SORTED_TILES"))
    NP = HD * (HD + 1) // 2
    FULL = HD // 2
    EXT = HD + FULL
    HB = B // 2
    ROWS = LB * B
    QUARTERED = [LB - 1]
    no = lambda pair, u: 2 * pair + u + 1
    with ExitStack() as c:
        sb = lambda n, sh, dt=F32: c.enter_context(nc.sbuf_tensor("a_" + n, sh, dt))
        psum = lambda n, sh: c.enter_context(nc.psum_tensor("a_" + n, sh, F32))
        sem = lambda n: c.enter_context(nc.semaphore("a_" + n))
        sems = lambda n: [sem(f"{n}{u}") for u in range(2)]
        gate_sb = sb("gate", [P, LB, E])
        zero = sb("zero", [P, L])
        x_in, x_again, c_in, c_rev, qn = (sb(n, [P, 2, L]) for n in ("x_in", "x_again", "c_in", "c_rev", "qn"))
        toep_hi, toep_lo = sb("toep_hi", [P, 2, L], F32R), sb("toep_lo", [P, 2, L], F32R)
        kext, qext = sb("kext", [P, 2, ROWS, EXT]), sb("qext", [P, 2, ROWS, EXT])
        kv = sb("kv", [P, 2, ROWS, NP])
        kv_hi, kv_lo = sb("kv_hi", [P, 2, ROWS, NP], F32R), sb("kv_lo", [P, 2, ROWS, NP], F32R)
        prods = sb("prods", [P, LB, B, HD, HD])
        halves = sb("halves", [P, 2, LB, FULL, B * HD])
        x2, xn = sb("x2", [P, 2, L]), sb("xn", [P, 2, L])
        xnT = sb("xnT", [P, 2, LB * P])
        xT = sb("xT", [P, 2, 2, LB * P], F16)
        stats, moments = sb("stats", [P, 2, 2, 6]), sb("moments", [P, 2, 2, 2])
        var_eps, rstd = sb("var_eps", [P, 2, 2, 1]), sb("rstd", [P, 2, 2, 1])
        power = sb("power", [P, 1])
        ps_y = [psum(f"ps_y{v}", [P, 2, 512]) for v in range(2)]
        ps_in = psum("ps_in", [P, LB * P])
        ps_sum = psum("ps_sum", [P, LB * P])
        ps_t = psum("ps_t", [P, LB * P])
        ps_l = psum("ps_l", [P, 512])
        x_loaded, c_loaded, again_loaded, toep_loaded = (sems(n) for n in ("x_loaded", "c_loaded", "again_loaded", "toep_loaded"))
        x2_stored, xn_stored, xT_stored = sems("x2_stored"), sems("xn_stored"), sems("xT_stored")
        gate_loaded, filled, zeroed = sem("gate_loaded"), sem("filled"), sem("zeroed")
        q_stats, q_moments, q_eps, q_rstd, q_done = (sem("q_" + n) for n in ("stats", "moments", "eps", "rstd", "done"))
        n_stats, n_moments, n_eps, n_rstd = (sem("n_" + n) for n in ("stats", "moments", "eps", "rstd"))
        c_rev_done, c_turned, q_turned, kext_done, qext_done = (sem(n) for n in ("c_rev", "c_turned", "q_turned", "kext", "qext"))
        kv_done, kv_hi_done, kv_lo_done = (sem(n) for n in ("kv", "kv_hi", "kv_lo"))
        y_done, prods_done, halved, halves_done, summed = (sem(n) for n in ("y", "prods", "halved", "halves", "summed"))
        x2_done, xn_done, xn_turned, xnT_done, xT_lo_done = (sem(n) for n in ("x2", "xn", "xn_turned", "xnT", "xT_lo"))
        logits_done, logits_kept = sem("logits"), sem("logits_kept")
        router = Router(nc, c, s, logits, slots, tops, tile_expert, ps_in, ps_sum)
        block = c.enter_context(nc.Block())
        PIECES = {1: 0, 3: 1, 5: 2, 7: 3, H: 4, H + 2: 5}

        def piece_at(what, turn, k):
            if not isinstance(turn, int):
                return None
            n = PIECES.get(2 * turn + k - (what in ("reduce", "scale", "high", "low")))
            return None if n is None else divmod(n, 3)

        split = SplitPieces(nc, c, s, *shared_w, piece_at, "a_w_")
        beside = lambda eng, work: (None, lambda turn, k: work(eng, turn, k))

        def rows_of(a, pair, u):
            h = 2 * pair + u
            return a[:, bass.ds(HD * h, HD), :]

        @block.sync
        def _(sp):
            sp.dma_start(gate_sb[:, :, :], gate_w.rearrange("(a p) e -> p a e", p=P)).then_inc(gate_loaded, 16)

            def load_c(pair, u):
                sp.wait_ge(c_rev_done, no(pair, u))
                sp.dma_start(c_in[:, u, :], rows_of(ctx_in, pair, u)).then_inc(c_loaded[u], 16)
                sp.wait_ge(q_done, no(pair, u))
                sp.dma_start(x_in[:, u, :], rows_of(x, pair, u)).then_inc(x_loaded[u], 16)

            def load_kernel(pair, u):
                sp.wait_ge(y_done, LB * no(pair, u))
                for part, dst in enumerate((toep_hi, toep_lo)):
                    src = bass.AP(kpad, (part * H + 2 * pair + u) * (P + L) + 1, [[1, P], [1, L]])
                    sp.dma_start(dst[:, u, :].bitcast(F32), src).then_inc(toep_loaded[u], 16)

            def fill(pair, u):
                for k in range(2):
                    sp.dma_start(xsort[bass.ds((2 * (2 * pair + u) + k) * P, P), :], zero[:, :]).then_inc(filled, 16)

            def load_again(pair, u):
                sp.wait_ge(x2_done, no(pair, u))
                sp.dma_start(x_again[:, u, :], rows_of(x, pair, u)).then_inc(again_loaded[u], 16)

            def store_x2(pair, u):
                sp.wait_ge(x2_done, no(pair, u) + 2)
                pass_waits(sp, s)
                sp.dma_start(x2_dram[bass.ds((2 * pair + u) * P, P), :], x2[:, u, :]).then_inc(x2_stored[u], 16)

            def store_xn(pair, u):
                sp.wait_ge(xn_done, no(pair, u) + 2)
                pass_waits(sp, s)
                sp.dma_start(xn_dram[bass.ds((2 * pair + u) * P, P), :], xn[:, u, :]).then_inc(xn_stored[u], 16)

            def store_xT(pair, u):
                sp.wait_ge(xT_lo_done, no(pair, u) + 2)
                pass_waits(sp, s)
                sp.dma_start(xT_dram[bass.ds((2 * pair + u) * P, P), :], xT[:, u, :, :].rearrange("p a t -> p (a t)"))\
                  .then_inc(xT_stored[u], 16)

            sp.wait_ge(zeroed, 2)
            run_skewed(sp, H, [(0, load_c), (0, fill), (2, load_again), (5, store_x2), (6, store_xn),
                               (8, store_xT), (1, load_kernel)], peeled=5)
            for t in range(2 * H, NT):
                sp.dma_start(xsort[t * P:(t + 1) * P, :], zero[:, :]).then_inc(filled, 16)
            sp.wait_ge(filled, 16 * NT)
            for u in range(2):
                sp.wait_ge(x2_stored[u], 16 * (H // 2 + 1))
                sp.wait_ge(xn_stored[u], 16 * (H // 2 + 1))
                sp.wait_ge(xT_stored[u], 16 * (H // 2 + 1))

        @block.gpsimd
        def _(pool):
            pool.memset(zero[:, :], 0.0).then_inc(zeroed, 1)
            pool.memset(power[:, :], -0.5).then_inc(zeroed, 1)
            router.draw(pool)
            for u in range(2):
                pool.sem_inc(x2_stored[u], 16)
                pool.sem_inc(xn_stored[u], 16)
                pool.sem_inc(xT_stored[u], 16)
            pool.sem_inc(kv_lo_done, 2)
            pool.sem_inc(halves_done, LB)
            pool.wait_ge(zeroed, 2)

            def rstd_of(which, moments_done, eps_done, rstd_done):
                def stage(pair, u):
                    n = no(pair, u)
                    pool.wait_ge(moments_done, n)
                    pass_waits(pool, s)
                    pool.tensor_scalar(var_eps[:, which, u, :], moments[:, which, u, 1:2], EPS, None, ALU.add)\
                        .then_inc(eps_done, 1)
                    pool.wait_ge(eps_done, n)
                    pool.tensor_tensor(rstd[:, which, u, :], var_eps[:, which, u, :], power[:, :], ALU.pow)\
                        .then_inc(rstd_done, 1)
                return stage

            def low(pair, u):
                n = no(pair, u)
                pool.wait_ge(y_done, LB * n)
                pool.wait_ge(kv_hi_done, n)
                pool.tensor_tensor(kv_lo[:, u, :, :], kv[:, u, :, :], kv_hi[:, u, :, :].bitcast(F32), ALU.subtract)\
                    .then_inc(kv_lo_done, 1)

            def add_halves(lbs):
                def stage(pair, u):
                    h = 2 * pair + u
                    if lbs[0] == 0:
                        pool.wait_ge(summed, no(pair, u))
                    for lb in lbs:
                        pool.wait_ge(prods_done, LB * h + lb + 1 + LB + 2)
                        pr = prods[:, lb, :, :, :].rearrange("p b s j -> p s b j")
                        half = halves[:, u, lb, :, :]
                        add = pool.tensor_tensor(half.rearrange("p s (b j) -> p s b j", j=HD), pr[:, 0:FULL],
                                                 pr[:, FULL:HD], ALU.add)
                        if lb in QUARTERED:
                            add.then_inc(halved, 1)
                            pool.wait_ge(halved, len(QUARTERED) * h + QUARTERED.index(lb) + 1)
                            add = pool.tensor_tensor(half[:, 0:FULL // 2], half[:, 0:FULL // 2], half[:, FULL // 2:FULL], ALU.add)
                        add.then_inc(halves_done, 1)
                return stage

            run_skewed(pool, H, [beside(pool, split.load), beside(pool, split.reduce),
                                 (1, rstd_of(0, q_moments, q_eps, q_rstd)),
                                 (5, rstd_of(1, n_moments, n_eps, n_rstd)), (1, low), (2, add_halves((0, 1))),
                                 (2, add_halves((2, 3)))], peeled=5)

        @block.tensor
        def _(pe):
            pe.sem_inc(c_turned, 2)
            pe.sem_inc(q_turned, 2)
            pe.sem_inc(y_done, 2 * LB)
            pe.sem_inc(summed, 2)
            pe.sem_inc(xn_turned, 2)
            pe.sem_inc(logits_done, 2)
            pe.wait_ge(gate_loaded, 16)

            def turn(src, u):
                for lb in range(LB):
                    mm = pe.transpose(ps_in[:, lb * P:(lb + 1) * P], src(lb), ident[:, :])
                return mm

            def turn_c(pair, u):
                n = no(pair, u)
                pe.wait_ge(c_rev_done, n + 2)
                pe.wait_ge(qext_done, n)
                turn(lambda lb: c_rev[:, u, (LB - 1 - lb) * P:(LB - lb) * P], u).then_inc(c_turned, 1)

            def turn_q(pair, u):
                n = no(pair, u)
                pe.wait_ge(q_done, n + 2)
                pe.wait_ge(kext_done, n + 2 + 1)
                turn(lambda lb: qn[:, u, lb * P:(lb + 1) * P], u).then_inc(q_turned, 1)

            def turn_last_q(pair, u):
                pe.wait_ge(q_done, no(pair, u) + 2)
                pe.wait_ge(qext_done, no(pair, u) + 1)
                turn(lambda lb: qn[:, u, lb * P:(lb + 1) * P], u).then_inc(q_turned, 1)

            def convolve(lbs):
                def stage(pair, u):
                    h = 2 * pair + u
                    pe.wait_ge(toep_loaded[u], 32 * pair + 32)
                    pe.wait_ge(kv_lo_done, h + 1 + 2)
                    for lb in lbs:
                        pe.wait_ge(prods_done, LB * h + lb + 1 + LB)
                        for half in range(2):
                            out = ps_y[lb % 2][:, half, 0:HB * NP]
                            for ib in range(lb + 1):
                                t = slice((lb - ib) * P, (lb - ib + 1) * P)
                                r = slice(ib * B + half * HB, ib * B + (half + 1) * HB)
                                for k, (w, m) in enumerate(((toep_hi, kv_hi), (toep_hi, kv_lo), (toep_lo, kv_hi))):
                                    mm = pe.matmul(out, w[:, u, t], m[:, u, r, :].rearrange("p b n -> p (b n)"),
                                                   start=(ib == 0 and k == 0), stop=(ib == lb and k == 2))
                        mm.then_inc(y_done, 1)
                return stage

            def sum_terms(pair, u):
                h = 2 * pair + u
                pe.wait_ge(x2_done, h + 2)
                pe.wait_ge(halves_done, LB * (h + 1) + LB)
                for lb in range(LB):
                    terms = FULL // 2 if lb in QUARTERED else FULL
                    for k in range(terms):
                        mm = pe.matmul(ps_sum[:, lb * P:(lb + 1) * P], halves[:, u, lb, k, :], ident[:, :],
                                       start=(k == 0), stop=(k == terms - 1))
                mm.then_inc(summed, 1)

            def turn_normed(pair, u):
                n = no(pair, u)
                pe.wait_ge(xn_done, n + 2)
                pe.wait_ge(xnT_done, n + 1)
                for lb in range(LB):
                    mm = pe.transpose(ps_t[:, lb * P:(lb + 1) * P], xn[:, u, lb * P:(lb + 1) * P], ident[:, :])
                mm.then_inc(xn_turned, 1)

            def route_logits(pair, u):
                n = no(pair, u)
                pe.wait_ge(xnT_done, n + 2)
                pe.wait_ge(logits_kept, n + 1)
                for lb in range(LB):
                    mm = pe.matmul(ps_l[:, 0:E], xnT[:, u, lb * P:(lb + 1) * P], gate_sb[:, lb, :], start=(lb == 0), stop=(lb == LB - 1))
                mm.then_inc(logits_done, 1)

            def q_stage(pair, u):
                last = isinstance(pair, int) and 2 * pair + u == H - 1
                (turn_last_q if last else turn_q)(pair, u)

            run_skewed(pe, H, [(2, convolve((0, 1))), (0, turn_c), (6, turn_normed), (7, route_logits), (2, convolve((2, 3))),
                               (1, q_stage), (3, sum_terms)])
            router.count(pe)

        @block.scalar
        def _(act):
            act.sem_inc(c_rev_done, 2)
            act.sem_inc(kext_done, 2)
            act.sem_inc(qext_done, 2)
            act.sem_inc(xnT_done, 2)

            def backwards(pair, u):
                act.wait_ge(c_loaded[u], 16 * pair + 16)
                act.wait_ge(c_turned, no(pair, u))
                whole = c_in[:, u, L - 1:L]
                act.activation(c_rev[:, u, :], bass.AP(whole.tensor, whole.offset, [whole.ap[0], [-1, L]]), ACT.Copy)\
                   .then_inc(c_rev_done, 1)

            def high(pair, u):
                n = no(pair, u)
                act.wait_ge(y_done, LB * n)
                act.wait_ge(kv_done, n + 2)
                act.activation(kv_hi[:, u, :, :], kv[:, u, :, :], ACT.Copy).then_inc(kv_hi_done, 1)

            def extend(dst, src, u, done):
                rows = src[:, :].rearrange("p (r j) -> p r j", j=HD)
                act.activation(dst[:, u, :, 0:HD], rows, ACT.Copy)
                act.activation(dst[:, u, :, HD:EXT], rows[:, :, 0:FULL], ACT.Copy).then_inc(done, 1)

            def extend_k(pair, u):
                act.wait_ge(c_turned, no(pair, u) + 2)
                act.wait_ge(kv_done, no(pair, u))
                extend(kext, ps_in, u, kext_done)

            def extend_q(pair, u):
                act.wait_ge(q_turned, no(pair, u) + 2)
                act.wait_ge(prods_done, LB * (2 * pair + u) + 2)
                extend(qext, ps_in, u, qext_done)

            def keep_turned(pair, u):
                n = no(pair, u)
                act.wait_ge(xn_turned, n + 2)
                act.wait_ge(logits_done, n)
                act.wait_ge(xT_lo_done, n)
                act.activation(xnT[:, u, :], ps_t[:, :], ACT.Copy)
                act.wait_ge(xT_stored[u], 16 * pair + 16)
                act.activation(xT[:, u, 0, :], ps_t[:, :], ACT.Copy, scale=X_SCALE).then_inc(xnT_done, 1)

            run_skewed(act, H, [(0, backwards), (1, high), (0, extend_k), beside(act, split.high),
                                (6, keep_turned), (1, extend_q)], peeled=5)
            router.exponents(act)

        @block.vector
        def _(dve):
            dve.sem_inc(kv_done, 2)
            dve.sem_inc(q_done, 2)
            dve.sem_inc(prods_done, LB + 2)
            dve.sem_inc(x2_done, 2)
            dve.sem_inc(xn_done, 2)
            dve.sem_inc(xT_lo_done, 2)
            dve.sem_inc(logits_kept, 2)

            def statistics(which, src, u, n, stats_done, moments_done):
                dve.bn_stats(stats[:, which, u, :], src).then_inc(stats_done, 1)
                dve.wait_ge(stats_done, n)
                pass_waits(dve, s)
                dve.bn_aggr(moments[:, which, u, :], stats[:, which, u, :]).then_inc(moments_done, 1)

            def add_x(pair, u):
                n = no(pair, u)
                dve.wait_ge(summed, n + 2)
                dve.wait_ge(again_loaded[u], 16 * pair + 16)
                dve.wait_ge(x2_stored[u], 16 * pair + 16)
                dve.wait_ge(xn_done, n)
                dve.tensor_tensor(x2[:, u, :], ps_sum[:, :], x_again[:, u, :], ALU.add).then_inc(x2_done, 1)

            def read_x2(pair, u):
                n = no(pair, u)
                dve.wait_ge(x2_done, n + 2)
                statistics(1, x2[:, u, :], u, n, n_stats, n_moments)

            def read_x(pair, u):
                dve.wait_ge(x_loaded[u], 16 * pair + 16)
                statistics(0, x_in[:, u, :], u, no(pair, u), q_stats, q_moments)

            def products(pair, u):
                n = no(pair, u)
                dve.wait_ge(kext_done, n + 2)
                dve.wait_ge(kv_lo_done, n)
                ke = kext[:, u, :, :]
                first = bass.AP(ke.tensor, ke.offset, [ke.ap[0], [EXT, ROWS], [0, FULL], [1, HD]])
                second = bass.AP(ke.tensor, ke.offset, [ke.ap[0], [EXT, ROWS], [1, FULL], [1, HD]])
                dve.tensor_tensor(kv[:, u, :, 0:FULL * HD].rearrange("p r (d j) -> p r d j", d=FULL), first, second, ALU.mult)
                dve.tensor_tensor(kv[:, u, :, FULL * HD:NP], ke[:, :, 0:FULL], ke[:, :, FULL:HD], ALU.mult)\
                   .then_inc(kv_done, 1)

            def norm_q(pair, u):
                n = no(pair, u)
                dve.wait_ge(q_rstd, n)
                dve.wait_ge(q_turned, n)
                dve.tensor_scalar(qn[:, u, :], x_in[:, u, :], moments[:, 0, u, 0:1], rstd[:, 0, u, :],
                                  ALU.subtract, ALU.mult).then_inc(q_done, 1)

            def norm_x2(pair, u):
                n = no(pair, u)
                dve.wait_ge(n_rstd, n)
                dve.wait_ge(xn_turned, n)
                dve.wait_ge(xn_stored[u], 16 * pair + 16)
                dve.tensor_scalar(xn[:, u, :], x2[:, u, :], moments[:, 1, u, 0:1], rstd[:, 1, u, :],
                                  ALU.subtract, ALU.mult).then_inc(xn_done, 1)

            def low_turned(pair, u):
                dve.wait_ge(xnT_done, no(pair, u) + 2)
                dve.scalar_tensor_tensor(xT[:, u, 1, :], xnT[:, u, :], X_SCALE, xT[:, u, 0, :], ALU.mult,
                                         ALU.subtract).then_inc(xT_lo_done, 1)

            def keep_logits(pair, u):
                dve.wait_ge(logits_done, no(pair, u) + 2)
                dve.tensor_copy(logits[:, bass.ds(2 * pair + u, 1), :].rearrange("p a e -> p (a e)"), ps_l[:, 0:E])\
                   .then_inc(logits_kept, 1)

            def weigh(lbs):
                def stage(pair, u):
                    h = 2 * pair + u
                    dve.wait_ge(qext_done, h + 1 + 2)
                    for lb in lbs:
                        m = LB * h + lb
                        y = ps_y[lb % 2][:, :, 0:HB * NP]
                        q = qext[:, u, lb * B:(lb + 1) * B, :]
                        pr = prods[:, lb, :, :, :]
                        dve.wait_ge(y_done, m + 1 + 2 * LB)
                        dve.wait_ge(halves_done, m + 1)
                        at = lambda a, off, outer, inner, dims: bass.AP(a.tensor, a.offset + off, [a.ap[0], [outer, 2], [inner, HB]] + dims)
                        yat = lambda off, dims: at(y, off, 512, NP, dims)
                        qat = lambda off, dims: at(q, off, EXT * HB, EXT, dims)
                        pat = lambda off, dims: at(pr, off, HD * HD * HB, HD * HD, dims)
                        dve.tensor_tensor(pat(0, [[HD, FULL], [1, HD]]), yat(0, [[HD, FULL], [1, HD]]),
                                          qat(0, [[1, FULL], [1, HD]]), ALU.mult)
                        dve.tensor_tensor(pat(FULL * HD + 1, [[HD + 1, FULL - 1], [1, HD]]),
                                          yat(HD, [[HD, FULL - 1], [1, HD]]),
                                          qat(0, [[0, FULL - 1], [1, HD]]), ALU.mult)
                        dve.tensor_tensor(pat(FULL * HD, [[HD + 1, FULL]]), yat(FULL * HD, [[1, FULL]]),
                                          qat(FULL, [[1, FULL]]), ALU.mult)
                        dve.tensor_tensor(pat(HD * HD - FULL, [[1, FULL]]), yat(FULL * HD, [[1, FULL]]),
                                          qat(0, [[1, FULL]]), ALU.mult).then_inc(prods_done, 1)
                return stage

            run_skewed(dve, H, [(8, keep_logits), (1, products), beside(dve, split.scale_of), (2, weigh((0, 1))),
                                (4, add_x), (0, read_x), (4, read_x2), (1, norm_q), (5, norm_x2), (2, weigh((2, 3))),
                                (7, low_turned), beside(dve, split.peaks_of), beside(dve, split.low_of)], peeled=5)
            dve.wait_ge(logits_kept, H + 2)
            router.choose(dve)


def expert_tiles(nc, s, kind, first, pairs, weights, scales, ident, ident16, tag, rows, y_dram=None, x2_dram=None,
                 unroll=2, expert_of=None, xn_dram=None, xsort=None, slots=None, tops=None, routed_w=None, out=None):
    LB, F, L, FB, TILES, HD = s["LB"], s["F"], s["L"], s["FB"], s["TILES"], s["HD"]
    LAST = F - (FB - 1) * P
    gu_hi, gu_lo, down_hi, down_lo = weights
    routed, shared, last = kind == "routed", kind == "shared", kind == "last"
    tiles = 2 * pairs
    XSLOTS = 2 if routed else unroll // 2
    with ExitStack() as c:
        sb = lambda n, sh, dt=F32: c.enter_context(nc.sbuf_tensor(tag + n, sh, dt))
        psum = lambda n, sh, dt=F32: c.enter_context(nc.psum_tensor(tag + n, sh, dt))
        sem = lambda n: c.enter_context(nc.semaphore(tag + n))
        xT = sb("xT", [P, XSLOTS, 2, LB, P], F16)
        gated = sb("gated", [P, 2, F])
        hid = sb("hid", [P, 2, F])
        hpeak, hinv, hscale, yscale = (sb(n, [P, 2, 1]) for n in ("hpeak", "hinv", "hscale", "yscale"))
        h16 = sb("h16", [P, 2, 2, F], F16)
        hT = sb("hT", [P, 2, 2, FB, P], F16)
        y = sb("y", [P, 2, L])
        ps_gu = [psum(f"ps_gu{u}", [P, 2, 512]) for u in range(2)]
        ps_h = psum("ps_h", [P, 2, FB, P], F16)
        ps_y = psum("ps_y", [P, 2, 512])
        loaded = [sem(f"loaded{u}") for u in range(XSLOTS)]
        stored = [sem(f"stored{u}") for u in range(2)]
        gate_done, up_done = sem("gate_done"), sem("up_done")
        gated_done, hid_done, small, h_hi_done, h_lo_done = (sem(n) for n in ("gated_done", "hid_done", "small", "h_hi", "h_lo"))
        yscale_done = sem("yscale_done")
        h_turned, hT_done, down_done, y_done = sem("h_turned"), sem("hT_done"), sem("down_done"), sem("y_done")
        if routed:
            x = sb("x", [P, 2, L])
            ps_x = psum("ps_x", [P, LB * P])
            x_turned, xT_hi_done, xT_done = sem("x_turned"), sem("xT_hi_done"), sem("xT_done")
        else:
            x2 = sb("x2", [P, L])
            x2_loaded = sem("x2_loaded")
        if shared:
            SENDS = TILES * unroll // tiles
            rows_at = sb("rows_at", [P, 2, 2], U32)
            sent = [sem(f"sent{i}") for i in range(2)]
            rows_done = sem("rows_done")
            to_send = sb("to_send", [P, 2, L])
            to_send_loaded = [sem(f"to_send_loaded{i}") for i in range(2)]
            split = SplitPieces(nc, c, s, *routed_w, lambda what, turn, k: (turn, k // 2)
                                if k % 2 == (what in ("reduce", "scale", "high", "low")) and not (isinstance(turn, int) and turn >= s["E"])
                                else None, tag + "w_")
        if last:
            order = []
            for step in range(tiles + 2):
                own = [first + (step - 3) // 2] if step % 2 and step >= 3 else []
                order += [(step, t) for t in own]
                early = sum(t < first for _, t in order)
                order += [(step, t) for t in range(early, min(early + (0 if step < 2 else 2 + (step == 4) - len(own)), first))]
            assert sorted(t for _, t in order) == list(range(TILES))
            SL = 6
            r = sb("r", [P, SL, L])
            g = sb("g", [P, SL, 2, L])
            acc = sb("acc", [P, SL, L])
            o = sb("o", [P, SL, L])
            r_loaded, g_loaded, out_stored = ([sem(f"{n}{u}") for u in range(SL)] for n in ("r_loaded", "g_loaded", "out_stored"))
            first_done, out_done = sem("first_done"), sem("out_done")
        peeled = tiles // unroll if last else 0
        beside = lambda eng, work: (None, lambda turn, k: work(eng, turn, k))
        block = c.enter_context(nc.Block())

        slot = lambda w: w % 2
        no = lambda turn, w: unroll * turn + w + 1
        pair_of = lambda turn, w: turn * (unroll // 2) + w // 2
        at_expert = lambda eng, turn, w: expert_of(eng, turn, w) if routed else w % 2
        x_slot = lambda w: w if routed else w // 2
        x_fills = lambda turn: turn + 1

        @block.sync
        def _(sp):
            def load(turn, w):
                if routed:
                    sp.wait_ge(x_turned, no(turn, w))
                    sp.dma_start(x[:, w, :], rows[bass.ds((unroll * turn + w) * P, P), :]).then_inc(loaded[w], 16)
                elif w % 2 == 0:
                    sp.wait_ge(up_done, unroll * turn + w + 2)
                    sp.dma_start(xT[:, w // 2, :, :, :].rearrange("p a b t -> p (a b t)"),
                                 rows[bass.ds((first + pair_of(turn, w)) * P, P), :]).then_inc(loaded[w // 2], 16)

            def load_to_send(turn, k):
                for i in range(SENDS):
                    if i * unroll // SENDS == k:
                        before = SENDS // 2 * turn + i // 2
                        if not (isinstance(turn, int) and before == 0):
                            sp.wait_ge(sent[i % 2], 32 * before)
                            pass_waits(sp, s)
                        sp.dma_start(to_send[:, i % 2, :], xn_dram[bass.ds((SENDS * turn + i) * P, P), :])\
                          .then_inc(to_send_loaded[i % 2], 16)

            def load_x2(turn, w):
                if not routed and w % 2 == 0:
                    sp.wait_ge(y_done, no(turn, w))
                    sp.dma_start(x2[:, :], x2_dram[bass.ds((first + pair_of(turn, w)) * P, P), :]).then_inc(x2_loaded, 16)

            def store(turn, w):
                if last or (shared and w % 2 == 0):
                    return
                sp.wait_ge(y_done, no(turn, w) + 2)
                pass_waits(sp, s)
                dst = y_dram[bass.ds((unroll * turn + w) * P, P), :] if routed else \
                    x2_dram[bass.ds((first + pair_of(turn, w)) * P, P), :]
                sp.dma_start(dst, y[:, w % 2, :]).then_inc(stored[w % 2], 16)

            def put_out(turn, k):
                for m, (step, t) in enumerate(order):
                    if step == unroll * turn + k - 1:
                        sp.wait_ge(out_done, m + 1)
                        sp.dma_start(out[:, t * HD:(t + 1) * HD, :], o[:, m % SL, :]).then_inc(out_stored[m % SL], 16)

            def load_rows(turn, k):
                for m, (step, t) in enumerate(order):
                    if t < first and max(step - 2, 0) == unroll * turn + k:
                        if m >= SL:
                            sp.wait_ge(first_done, m - SL + 1)
                        sp.dma_start(r[:, m % SL, :], x2_dram[t * P:(t + 1) * P, :]).then_inc(r_loaded[m % SL], 16)

            if last:
                run_skewed(sp, tiles, [(0, load), (1, load_x2), (0, load_rows), (0, put_out)], unroll, peeled)
                put_out(tiles // unroll, 0)
                put_out(tiles // unroll, 1)
                put_out(tiles // unroll, 2)
                for u in range(SL):
                    sp.wait_ge(out_stored[u], 16 * len(range(u, TILES, SL)))
            else:
                for u in range(2):
                    sp.sem_inc(stored[u], 16)
                run_skewed(sp, tiles, [(0, load), (0, load_to_send), (1, load_x2), (4, store)] if shared else [(0, load), (4, store)], unroll)
                for u in range(2):
                    if routed or u == 1:
                        sp.wait_ge(stored[u], 16 * (tiles // 2) + 16)

        @block.gpsimd
        def _(pool):
            def send(turn, k):
                for i in range(SENDS):
                    if i * unroll // SENDS != k:
                        continue
                    t = SENDS * turn + i
                    before = SENDS // 2 * turn + i // 2
                    if not (isinstance(turn, int) and before == 0):
                        pool.wait_ge(sent[i % 2], 32 * before)
                        pass_waits(pool, s)
                    pool.tensor_copy(rows_at[:, i % 2, :], slots[:, :, bass.ds(t, 1)].rearrange("p k a -> p (k a)"))\
                        .then_inc(rows_done, 1)
                    pool.wait_ge(rows_done, t + 1)
                    pool.wait_ge(to_send_loaded[i % 2], 16 * before + 16)
                    pass_waits(pool, s)
                    for n in range(2):
                        pool.indirect_dma_start(
                            out=xsort[:, :], out_offset=bass.IndirectOffsetOnAxis(ap=rows_at[:, i % 2, n:n + 1], axis=0),
                            in_=to_send[:, i % 2, :], in_offset=None).then_inc(sent[i % 2], 16)

            if shared:
                run_skewed(pool, tiles, [beside(pool, split.load), beside(pool, split.reduce), (0, send)], unroll, 1)
                for i in range(2):
                    pool.wait_ge(sent[i], 32 * (TILES // 2))
            if last:
                for m, (_, t) in enumerate(order):
                    if m >= SL:
                        pool.wait_ge(out_done, m - SL + 1)
                    for k in range(2):
                        pool.indirect_dma_start(out=g[:, m % SL, k, :], out_offset=None, in_=y_dram[:, :],
                                                in_offset=bass.IndirectOffsetOnAxis(ap=slots[:, k, t:t + 1], axis=0))\
                            .then_inc(g_loaded[m % SL], 16)

        @block.tensor
        def _(pe):
            experts, down_expert = {}, {}

            def turn_x(turn, w):
                pe.wait_ge(loaded[w], 16 * x_fills(turn))
                pe.wait_ge(xT_done, no(turn, w) + 1)
                for lb in range(LB):
                    mm = pe.transpose(ps_x[:, lb * P:(lb + 1) * P], x[:, w, lb * P:(lb + 1) * P], ident[:, :])
                mm.then_inc(x_turned, 1)

            def project(w, k, done):
                e = experts[w % 2]
                out = ps_gu[w % 2][:, k, 0:F]
                for kb in range(LB):
                    for n, (a, b) in enumerate(((0, gu_hi), (0, gu_lo), (1, gu_hi))):
                        mm = pe.matmul(out, xT[:, x_slot(w), a, kb, :],
                                       b[:, bass.ds(e, 1), kb, k * F:(k + 1) * F].rearrange("p a f -> p (a f)"),
                                       start=(kb == 0 and n == 0), stop=(kb == LB - 1 and n == 2))
                mm.then_inc(done, 1)

            def gate(turn, w):
                experts[w % 2] = at_expert(pe, turn, w)
                if routed:
                    pe.wait_ge(xT_done, no(turn, w) + 2)
                elif w % 2 == 0:
                    pe.wait_ge(loaded[w // 2], 16 * x_fills(turn))
                pe.wait_ge(hid_done, no(turn, w))
                project(w, 0, gate_done)

            def up(turn, w):
                project(w, 1, up_done)

            def turn_h(turn, w):
                u = w % 2
                pe.wait_ge(h_lo_done, no(turn, w))
                pe.wait_ge(hT_done, no(turn, w) + 1)
                for part in range(2):
                    for fb in range(FB):
                        n = P if fb < FB - 1 else LAST
                        mm = pe.transpose(ps_h[0:n, part, fb, :], h16[:, u, part, fb * P:fb * P + n], ident16[:, :])
                mm.then_inc(h_turned, 1)

            def down(turn, w):
                u = w % 2
                e = at_expert(pe, turn, w)
                pe.wait_ge(hT_done, no(turn, w) + 2)
                pe.wait_ge(y_done, no(turn, w))
                for fb in range(FB):
                    n = P if fb < FB - 1 else LAST
                    for k, (a, b) in enumerate(((0, down_hi), (0, down_lo), (1, down_hi))):
                        mm = pe.matmul(ps_y[:, u, :], hT[0:n, u, a, fb, :],
                                       b[0:n, bass.ds(e, 1), fb, :].rearrange("p a f -> p (a f)"),
                                       start=(fb == 0 and k == 0), stop=(fb == FB - 1 and k == 2))
                mm.then_inc(down_done, 1)

            if routed:
                pe.sem_inc(x_turned, 2)
            run_skewed(pe, tiles, ([(0, turn_x)] if routed else []) + [(1, gate), (2, turn_h), (1, up), (2, down)], unroll)

        @block.scalar
        def _(act):
            def high_x(turn, w):
                act.wait_ge(x_turned, no(turn, w) + 2)
                act.wait_ge(up_done, no(turn, w))
                act.activation(xT[:, w, 0, :, :].rearrange("p b t -> p (b t)"), ps_x[:, :], ACT.Copy, scale=X_SCALE)\
                   .then_inc(xT_hi_done, 1)

            def swish(turn, w):
                u = w % 2
                e = at_expert(act, turn, w)
                act.wait_ge(gate_done, no(turn, w))
                act.wait_ge(hid_done, no(turn, w))
                act.activation(gated[:, u, :], ps_gu[u][:, 0, 0:F], ACT.Silu,
                               scale=scales[:, bass.ds(e, 1), 0:1].rearrange("p a k -> p (a k)")).then_inc(gated_done, 1)

            def high(turn, w):
                u = w % 2
                act.wait_ge(small, 3 * no(turn, w))
                act.wait_ge(h_turned, no(turn, w))
                act.activation(h16[:, u, 0, :], hid[:, u, :], ACT.Copy, scale=hscale[:, u, :]).then_inc(h_hi_done, 1)

            def keep_hT(turn, w):
                u = w % 2
                act.wait_ge(h_turned, no(turn, w) + 2)
                act.wait_ge(down_done, no(turn, w))
                act.activation(hT[:, u, :, 0:FB - 1, :], ps_h[:, :, 0:FB - 1, :], ACT.Copy)
                act.activation(hT[0:LAST, u, :, FB - 1, :], ps_h[0:LAST, :, FB - 1, :], ACT.Copy).then_inc(hT_done, 1)

            def result(turn, w):
                u = w % 2
                act.wait_ge(down_done, no(turn, w) + 2)
                act.wait_ge(yscale_done, no(turn, w))
                act.wait_ge(stored[u], 16 * turn + 16)
                act.activation(y[:, u, :], ps_y[:, u, :], ACT.Copy, scale=yscale[:, u, :]).then_inc(y_done, 1)

            act.sem_inc(hT_done, 2)
            if routed:
                act.sem_inc(y_done, 2)
            if routed:
                run_skewed(act, tiles, [(0, high_x), (2, keep_hT), (1, swish), (1, high), (2, result)])
            else:
                run_skewed(act, tiles, [(2, keep_hT), (1, swish), (1, high)] + ([beside(act, split.high)] if shared else []),
                           unroll)

        @block.vector
        def _(dve):
            def low_x(turn, w):
                dve.wait_ge(xT_hi_done, no(turn, w))
                flat = lambda a: xT[:, w, a, :, :].rearrange("p b t -> p (b t)")
                dve.scalar_tensor_tensor(flat(1), ps_x[:, :], X_SCALE, flat(0), ALU.mult, ALU.subtract).then_inc(xT_done, 1)

            def hidden(turn, w):
                u = w % 2
                e = at_expert(dve, turn, w)
                n = no(turn, w)
                dve.wait_ge(up_done, n + (2 if routed else unroll))
                dve.wait_ge(gated_done, n)
                dve.scalar_tensor_tensor(hid[:, u, :], ps_gu[u][:, 1, 0:F],
                                         scales[:, bass.ds(e, 1), 1:2].rearrange("p a k -> p (a k)"),
                                         gated[:, u, :], ALU.mult, ALU.mult).then_inc(hid_done, 1)
                dve.wait_ge(hid_done, n + 2)
                dve.tensor_reduce(hpeak[:, u, :], hid[:, u, :], AX.X, ALU.max, apply_absolute_value=True).then_inc(small, 1)
                dve.wait_ge(small, 3 * n - 2)
                dve.tensor_scalar(hinv[:, u, :], hpeak[:, u, :], TINY, 1.0 / PEAK, ALU.max, ALU.mult).then_inc(small, 1)
                dve.wait_ge(small, 3 * n - 1)
                dve.reciprocal(hscale[:, u, :], hinv[:, u, :]).then_inc(small, 1)
                dve.wait_ge(y_done, n)
                dve.tensor_tensor(yscale[:, u, :], hinv[:, u, :],
                                  scales[:, bass.ds(e, 1), 2:3].rearrange("p a k -> p (a k)"), ALU.mult)\
                   .then_inc(yscale_done, 1)

            def low(turn, w):
                u = w % 2
                dve.wait_ge(h_hi_done, no(turn, w))
                dve.scalar_tensor_tensor(h16[:, u, 1, :], hid[:, u, :], hscale[:, u, :], h16[:, u, 0, :], ALU.mult,
                                         ALU.subtract).then_inc(h_lo_done, 1)

            def put_together(m, t, base):
                dve.wait_ge(g_loaded[m % SL], 32 * (m // SL + 1))
                dve.scalar_tensor_tensor(acc[:, m % SL, :], g[:, m % SL, 0, :], tops[:, 0, t:t + 1], base, ALU.mult, ALU.add)\
                   .then_inc(first_done, 1)
                dve.wait_ge(first_done, m + 1)
                if m >= SL:
                    dve.wait_ge(out_stored[m % SL], 16 * (m // SL))
                dve.scalar_tensor_tensor(o[:, m % SL, :], g[:, m % SL, 1, :], tops[:, 1, t:t + 1], acc[:, m % SL, :],
                                         ALU.mult, ALU.add).then_inc(out_done, 1)

            def put_early(turn, k):
                for m, (step, t) in enumerate(order):
                    if t < first and step == unroll * turn + k:
                        dve.wait_ge(r_loaded[m % SL], 16 * sum(n % SL == m % SL and a < first for n, (_, a) in enumerate(order[:m + 1])))
                        put_together(m, t, r[:, m % SL, :])

            def result(turn, w):
                u = w % 2
                n = no(turn, w)
                dve.wait_ge(down_done, n + 2)
                dve.wait_ge(yscale_done, n)
                if u == 0:
                    dve.wait_ge(x2_loaded, 16 * pair_of(turn, w) + 16)
                    dve.wait_ge(y_done, n + 1)
                    src = x2[:, :]
                else:
                    dve.wait_ge(y_done, n + 1)
                    if shared:
                        dve.wait_ge(stored[1], 16 * pair_of(turn, w) + 16)
                    src = y[:, 0, :]
                dve.scalar_tensor_tensor(y[:, u, :], ps_y[:, u, :], yscale[:, u, :], src, ALU.mult, ALU.add)\
                   .then_inc(y_done, 1)
                if last and u == 1:
                    dve.wait_ge(y_done, n + 2)
                    t = first + pair_of(turn, w)
                    put_together([a for _, a in order].index(t), t, y[:, 1, :])

            dve.sem_inc(up_done, 2 if routed else unroll)
            dve.sem_inc(hid_done, 2)
            dve.sem_inc(h_turned, 2)
            dve.sem_inc(down_done, 2)
            if routed:
                dve.sem_inc(xT_done, 2)
                run_skewed(dve, tiles, [(0, low_x), (1, hidden), (1, low)], unroll)
            else:
                dve.sem_inc(y_done, 2)
                if shared:
                    run_skewed(dve, tiles, [(1, hidden), beside(dve, split.scale_of), (1, low), (2, result),
                                            beside(dve, split.peaks_of), beside(dve, split.low_of)], unroll)
                else:
                    run_skewed(dve, tiles, [(1, hidden), (1, low), (2, result), (None, put_early)], unroll, peeled)


def build(nc, x, ctx_in, ssm_kernel, dvec, gate_w, w_gate, w_up, w_down, sw_gate, sw_up, sw_down, out):
    s = shapes_of(x, ssm_kernel, gate_w, w_gate)
    B, L, LB, H, HD, E, F, TILES = (s[k] for k in ("B", "L", "LB", "H", "HD", "E", "F", "TILES"))
    s["FB"] = -(-F // P)
    s["SORTED_TILES"] = 2 * TILES + E
    s["LAST_TILES"] = TILES - 3 * E
    kpad = nc.dram_tensor("kpad", [2, H, P + L], F32)
    x2_dram = nc.dram_tensor("x2_rows", [s["TOKENS"], L], F32)
    xn_dram = nc.dram_tensor("xn_rows", [s["TOKENS"], L], F32)
    xT_dram = nc.dram_tensor("xT_rows", [s["TOKENS"], 2 * L], F16)
    xsort = nc.dram_tensor("x_sorted", [s["SORTED_TILES"] * P, L], F32)
    y_dram = nc.dram_tensor("y_sorted", [s["SORTED_TILES"] * P, L], F32)
    whole = (s["FB"] - 1) * P

    def in_parts(kind, w):
        if kind < 2:
            return [w.rearrange("(c p) f -> p c f", p=P)]
        return [w[0:whole, :].rearrange("(c p) l -> p c l", p=P), w[whole:F, :].rearrange("(c p) l -> p c l", c=1)]

    def shared_sources(kind, e):
        half = slice(e * F, (e + 1) * F)
        return in_parts(kind, sw_down[half, :] if kind == 2 else (sw_gate, sw_up)[kind][:, half])

    def routed_sources(kind, e):
        return in_parts(kind, (w_gate, w_up, w_down)[kind][bass.ds(e, 1), :, :].rearrange("a k n -> (a k) n"))

    with ExitStack() as c:
        sb = lambda n, sh, dt=F32: c.enter_context(nc.sbuf_tensor(n, sh, dt))
        ident, ident16 = identities(nc, s, c)
        logits = sb("logits", [P, TILES, E])
        tops = sb("tops", [P, 2, TILES])
        slots = sb("slots", [P, 2, TILES], U32)
        tile_expert = sb("tile_expert", [P, s["SORTED_TILES"]], I32)
        scales = sb("scales", [P, E, 3])
        shared_scales = sb("shared_scales", [P, 2, 3])

        def split_buffers(ctx, tag, n):
            return tuple(ctx.enter_context(nc.sbuf_tensor(tag + m, sh, F16)) for m, sh in (
                ("gu_hi", [P, n, LB, 2 * F]), ("gu_lo", [P, n, LB, 2 * F]),
                ("down_hi", [P, n, s["FB"], L]), ("down_lo", [P, n, s["FB"], L])))

        pad_kernels(nc, s, ssm_kernel, dvec, kpad)
        with ExitStack() as a:
            shared_parts = split_buffers(a, "shared_", 2)
            attention(nc, s, x, ctx_in, gate_w, kpad, x2_dram, xn_dram, xT_dram, xsort, logits, slots, tops, tile_expert, ident,
                      (shared_sources, shared_parts, shared_scales))
            common = dict(ident=ident, ident16=ident16)
            with ExitStack() as b:
                parts = split_buffers(b, "", E)
                expert_tiles(nc, s, "shared", 0, TILES - s["LAST_TILES"], shared_parts, shared_scales, tag="s_", rows=xT_dram,
                             x2_dram=x2_dram, unroll=6, xn_dram=xn_dram, xsort=xsort, slots=slots,
                             routed_w=(routed_sources, parts, scales), **common)
                expert_tiles(nc, s, "routed", 0, s["SORTED_TILES"] // 2, parts, scales, tag="e_", rows=xsort, y_dram=y_dram,
                             expert_of=lambda eng, pair, u: eng.value_load(tile_expert[0:1, bass.ds(2 * pair + u, 1)],
                                                                           min_val=0, max_val=E - 1), **common)
            expert_tiles(nc, s, "last", TILES - s["LAST_TILES"], s["LAST_TILES"], shared_parts, shared_scales, tag="l_",
                         rows=xT_dram, x2_dram=x2_dram, y_dram=y_dram, unroll=4, slots=slots, tops=tops, out=out, **common)


_INS = ["x", "ctx_2048", "L0_xattn_ssm_kernel", "L0_xattn_D", "L0_ffn_gate_w", "L0_ffn_w_gate", "L0_ffn_w_up",
        "L0_ffn_w_down", "L0_ffn_sw_gate", "L0_ffn_sw_up", "L0_ffn_sw_down"]


def kernel(**inputs):
    import numpy as _np
    import concourse.bacc as _bacc
    from concourse import mybir as _mybir
    from concourse.bass_utils import run_bass_kernel_spmd as _run

    nc = _bacc.Bacc("TRN2", target_bir_lowering=False, num_devices=1)
    arrays, args = {}, []
    for name in _INS:
        a = _np.ascontiguousarray(inputs[name])
        arrays[f"in_{name}"] = a
        args.append(nc.dram_tensor(f"in_{name}", a.shape, _mybir.dt.from_np(a.dtype), kind="ExternalInput").ap())
    shape = arrays["in_x"].shape
    args.append(nc.dram_tensor("out_0", shape, _mybir.dt.float32, kind="ExternalOutput").ap())
    build(nc, *args)
    r = _run(nc, [arrays], core_ids=[0])
    return r.results[0]["out_0"]
```
